# Optimizing a Trainium2 kernel written in Bass

```python
import numpy as np
import jax
import jax.numpy as jnp

def _softmax(x, axis=-1):
    return jax.nn.softmax(x, axis=axis)

def _gelu(x):
    return jax.nn.gelu(x, approximate=True)

def _silu(x):
    return jax.nn.silu(x)

def _sigmoid(x):
    return jax.nn.sigmoid(x)

def _layernorm(x, axis=-1, eps=1e-05):
    m = jnp.mean(x, axis=axis, keepdims=True)
    v = jnp.var(x, axis=axis, keepdims=True)
    return (x - m) / jnp.sqrt(v + eps)

def _scatter_add(tgt, idx, src, axis=0):
    return tgt.at[idx].add(src)

def _segment_sum(src, seg, n):
    return jax.ops.segment_sum(src, seg, n)
kernel_name = 'mk_gnn_preln_d2_gnn_r8_da5cb5'

def setup_inputs(seed: int=0):
    np.random.seed(seed)
    _w = jnp.asarray

    def _rec_inputs():
        import jax
        import jax.numpy as jnp
        _gk = jax.random.key(seed)
        x = -0.0001006 + 1 * jax.random.normal(jax.random.fold_in(_gk, 1), (6250, 96), jnp.float32)
        src = jax.random.randint(jax.random.fold_in(_gk, 2), (100000,), 0, 6250, jnp.int32)
        dst = jnp.minimum((6250 * jax.random.uniform(jax.random.fold_in(_gk, 3), (100000,)) ** 2.0).astype(jnp.int32), 49999)
        _o = jnp.argsort(dst, stable=True)
        src = src[_o]
        dst = dst[_o]
        return (x, src, dst)
    x, src, dst = _rec_inputs()

    def _L0_gnn_setup():
        import jax, jax.numpy as jnp
        import numpy as np
        N_NODES = 6250
        N_EDGES = 100000
        IN_FEATS = 96
        OUT_FEATS = 96
        EPS = 1e-08
        key = jax.random.key(seed)
        k1, k2, k3, k4, k5 = jax.random.split(key, 5)
        feat = jax.random.normal(k1, (N_NODES, IN_FEATS), dtype=jnp.float32)
        src = jax.random.randint(k2, (N_EDGES,), 0, N_NODES, dtype=jnp.int32)
        dst = jax.random.randint(k3, (N_EDGES,), 0, N_NODES, dtype=jnp.int32)
        edge_index = jnp.stack([src, dst], axis=0)
        gain = float(np.sqrt(2.0))
        bound = gain * float(np.sqrt(6.0 / (IN_FEATS + OUT_FEATS)))
        W_self = jax.random.uniform(k4, (OUT_FEATS, IN_FEATS), minval=-bound, maxval=bound, dtype=jnp.float32)
        W_neigh = jax.random.uniform(k5, (OUT_FEATS, IN_FEATS), minval=-bound, maxval=bound, dtype=jnp.float32)
        return {'feat': feat, 'edge_index': edge_index, 'W_self': W_self, 'W_neigh': W_neigh}
    _L0_gnn_all = _L0_gnn_setup()
    _L0_gnn_in = {k: v for k, v in _L0_gnn_all.items() if k in ('W_self', 'W_neigh')}
    del _L0_gnn_all

    def _L1_gnn_setup():
        import jax, jax.numpy as jnp
        import numpy as np
        N_NODES = 6250
        N_EDGES = 100000
        D_MODEL = 96
        HEADS = 4
        key = jax.random.key(seed)
        ks = jax.random.split(key, 6)
        scale = 1.0 / np.sqrt(D_MODEL)
        return {'embeds': jax.random.normal(ks[0], (N_NODES, D_MODEL), dtype=jnp.float32), 'qW': jax.random.normal(ks[1], (D_MODEL, D_MODEL), dtype=jnp.float32) * scale, 'kW': jax.random.normal(ks[2], (D_MODEL, D_MODEL), dtype=jnp.float32) * scale, 'vW': jax.random.normal(ks[3], (D_MODEL, D_MODEL), dtype=jnp.float32) * scale, 'rows': jax.random.randint(ks[4], (N_EDGES,), 0, N_NODES, dtype=jnp.int32), 'cols': jax.random.randint(ks[5], (N_EDGES,), 0, N_NODES, dtype=jnp.int32)}
    _L1_gnn_all = _L1_gnn_setup()
    _L1_gnn_in = {k: v for k, v in _L1_gnn_all.items() if k in ('qW', 'kW', 'vW')}
    del _L1_gnn_all
    return {'x': x, 'src': src, 'dst': dst, 'L0_gnn_W_self': _L0_gnn_in['W_self'], 'L0_gnn_W_neigh': _L0_gnn_in['W_neigh'], 'L1_gnn_qW': _L1_gnn_in['qW'], 'L1_gnn_kW': _L1_gnn_in['kW'], 'L1_gnn_vW': _L1_gnn_in['vW']}

def reference(x, src, dst, L0_gnn_W_self, L0_gnn_W_neigh, L1_gnn_qW, L1_gnn_kW, L1_gnn_vW):
    import jax
    import jax.numpy as jnp

    def _L0_gnn_ref(feat, edge_index, W_self, W_neigh):
        import jax, jax.numpy as jnp
        import numpy as np
        N_NODES = 6250
        N_EDGES = 100000
        IN_FEATS = 96
        OUT_FEATS = 96
        EPS = 1e-08
        src = edge_index[0]
        dst = edge_index[1]
        msgs = feat[src]
        neigh_sum = jax.ops.segment_sum(msgs, dst, num_segments=N_NODES)
        degs = jax.ops.segment_sum(jnp.ones((edge_index.shape[1],), jnp.float32), dst, num_segments=N_NODES)
        h_neigh = (neigh_sum + EPS) / (degs[:, None] + EPS)
        rst = feat @ W_self.T + h_neigh @ W_neigh.T
        return rst

    def _L1_gnn_ref(embeds, qW, kW, vW, rows, cols):
        import jax, jax.numpy as jnp
        import numpy as np
        N_NODES = 6250
        N_EDGES = 100000
        D_MODEL = 96
        HEADS = 4
        nvar, d = embeds.shape
        dh = d // HEADS
        e = rows.shape[0]
        q = (embeds[rows] @ qW).reshape(e, HEADS, dh)
        k = (embeds[cols] @ kW).reshape(e, HEADS, dh)
        v = (embeds[cols] @ vW).reshape(e, HEADS, dh)
        scores = jnp.clip(jnp.einsum('ehd,ehd->eh', q, k), -10.0, 10.0)
        exp_s = jnp.exp(scores)
        norms = jax.ops.segment_sum(exp_s, rows, num_segments=nvar)[rows]
        w = exp_s / (norms + 1e-08)
        res = jax.ops.segment_sum(w[:, :, None] * v, rows, num_segments=nvar).reshape(nvar, d)
        return embeds + res
    edge_index = jnp.stack([src, dst])
    h = jnp.maximum(_layernorm(x, axis=-1), 0.0)
    x = x + _L0_gnn_ref(h, edge_index, L0_gnn_W_self, L0_gnn_W_neigh)
    h = jnp.maximum(_layernorm(x, axis=-1), 0.0)
    x = x + _L1_gnn_ref(h, L1_gnn_qW, L1_gnn_kW, L1_gnn_vW, src, dst)
    return x

_drawn_inputs = setup_inputs


def setup_inputs(seed=0):
    import zlib

    import numpy as np

    out = dict(_drawn_inputs(seed))
    spreads = {}
    factors = {}
    for name, (base, spread) in spreads.items():
        noise = np.random.default_rng([zlib.crc32(name.encode()), seed]).standard_normal(out[name].shape)
        drawn = base * np.exp(spread * noise) if base else spread * noise
        out[name] = jnp.asarray(drawn.astype(out[name].dtype))
    for name, factor in factors.items():
        out[name] = (out[name] * factor).astype(out[name].dtype)
    return out
```

```python
import concourse.bass as bass
from concourse import mybir
from contextlib import ExitStack

P = 128
N_NODES = 6250
N_EDGES = 100000
D = 96
HEADS = 4
DH = D // HEADS
EPS_LN = 1e-5
EPS = 1e-8
NB = -(-N_NODES // P)
NPAD = NB * P
TAIL = N_NODES - (NB - 1) * P
BLK = -(-(-(-N_EDGES // P)) // P)
GT = 4
RAWT = -(-(-(-N_EDGES // P)) // GT) * GT
TILES = -(-((N_EDGES + NB * (P - 1)) // P) // GT) * GT
GROUPS = TILES // GT
CHUNKS = RAWT // GT
RING = 4
W0 = D + 1
W1 = D + HEADS
NT7 = 7
STEPS7 = NB // NT7
HALF = 512
assert NB % NT7 == 0 and GROUPS % RING == 0 and CHUNKS % RING == 0


def gnn_program(nc, x, src, dst, w_self, w_neigh, qw, kw, vw, h_table, kv_table, out):
    f32, i32, f16 = mybir.dt.float32, mybir.dt.int32, mybir.dt.float16
    ALU = mybir.AluOpType
    ACT = mybir.ActivationFunctionType
    X = mybir.AxisListType.X

    with ExitStack() as ctx:
        def sb(name, shape, dt):
            return ctx.enter_context(nc.sbuf_tensor(name, shape, dt))

        def sem(name):
            return ctx.enter_context(nc.semaphore(name))

        iota_part_i = sb("iota_part_i", [P, 1], i32)
        iota_h = sb("iota_h", [P, TILES], f16)
        iota_f = sb("iota_f", [P, P], f32)
        iota_part = sb("iota_part", [P, 1], f32)
        ident = sb("ident", [P, P], f32)
        before = sb("before", [P, P], f32)
        ones = sb("ones", [P, P], f32)
        ones_h = sb("ones_h", [P, 1], f16)
        eps_col = sb("eps_col", [P, 1], f32)
        zeros_h = sb("zeros_h", [P, P], f16)
        ones_row = sb("ones_row", [P, RAWT], f32)
        w_rows = sb("w_rows", [D, 2, D], f32)
        w_in = sb("w_in", [D, 2, D], f32)
        w_qkv = sb("w_qkv", [D, 3 * D], f32)
        edge = [sb("edge_src", [P, BLK * P], f32), sb("edge_dst", [P, BLK * P], f32)]
        ints = sb("ints", [P, TILES], i32)
        bucket = sb("bucket", [P, RAWT], f32)
        mask = sb("mask", [P, RAWT], f32)
        scan = sb("scan", [P, TILES], f32)
        position = sb("position", [P, RAWT], f32)
        cols = sb("cols", [P, RAWT, 4], f32)
        counts = sb("counts", [P, NB], f32)
        tiles_i = sb("tiles_i", [P, NB], i32)
        tiles_f = sb("tiles_f", [P, NB], f32)
        tiles_end = sb("tiles_end", [P, NB], f32)
        base = sb("base", [P, NB], f32)
        end_col = sb("end_col", [P, 1], f32)
        past_end = sb("past_end", [P, TILES], f16)
        tile_bucket = sb("tile_bucket", [1, TILES], i32)
        cols_stage = sb("cols_stage", [P, RING, GT, 4], f32)
        hot_tile = sb("hot_tile", [P, 2, GT, TILES], f16)
        hot_row = sb("hot_row", [P, 2, GT, 2, P], f16)
        other_idx = sb("other_idx", [P, TILES], i32)
        local = sb("local", [P, TILES], f32)
        xs = sb("xs", [P, NB, D], f32)
        h = sb("h", [P, NB, D], f32)
        work = sb("work", [P, NB, D], f32)
        q = sb("q", [P, NB, D], f32)
        stat = sb("stat", [P, NB], f32)
        stat2 = sb("stat2", [P, NB], f32)
        acc = sb("acc", [P, NB, W1], f32)
        rec = sb("rec", [P, NB, HEADS], f32)
        idx_stage = sb("idx_stage", [P, RING, GT], i32)
        loc_stage = sb("loc_stage", [P, RING, GT], f32)
        msg = sb("msg", [P, RING, GT, 2 * D], f32)
        one_col = sb("one_col", [P, 1], f32)
        hot = sb("hot", [P, RING, GT, P], f32)
        hot_t = sb("hot_t", [P, 2, GT, P], f32)
        prod = sb("prod", [P, GT, D], f32)
        score = sb("score", [P, 2, GT * HEADS], f32)
        weighted = sb("weighted", [P, 2, GT, W1], f32)
        node_t = sb("node_t", [D, 2, NT7, P], f32)

        spare = q[:, :, :].rearrange("p t f -> p (t f)")
        EDGES = 2 * BLK * P
        raw = spare[:, 0:EDGES].bitcast(i32).rearrange("p (k b e) -> p k b e", k=2, b=BLK)
        raw_f = spare[:, EDGES:2 * EDGES].rearrange("p (k b e) -> p k b e", k=2, b=BLK)
        iota_i = spare[:, 2 * EDGES:2 * EDGES + TILES].bitcast(i32)
        node_stage = hot[:, :, :, :].rearrange("p r g e -> p (r g e)")[:, 0:2 * NT7 * D].rearrange("p (k t f) -> p k t f", k=2, t=NT7)
        kv_stage = msg[:, :, :, :].rearrange("p r g f -> p (r g f)")[:, 0:4 * NT7 * D].rearrange("p (k t f) -> p k t f", k=2, t=NT7)

        psA = ctx.enter_context(nc.psum_tensor("psA", [P, 2 * HALF], f32))
        psB = ctx.enter_context(nc.psum_tensor("psB", [P, 2 * HALF], f32))
        psC = ctx.enter_context(nc.psum_tensor("psC", [P, 2 * HALF], f32))
        psD = ctx.enter_context(nc.psum_tensor("psD", [P, 2 * HALF], f32))

        s_raw_set = sem("s_raw_set")
        s_edges_in = sem("s_edges_in")
        s_x_set = sem("s_x_set")
        s_x_in = sem("s_x_in")
        s_w_in = sem("s_w_in")
        s_iota = sem("s_iota")
        s_const = sem("s_const")
        s_dve = sem("s_dve")
        s_raw_f = sem("s_raw_f")
        s_edge_t = sem("s_edge_t")
        s_edge = sem("s_edge")
        s_w_t = sem("s_w_t")
        s_w_ready = sem("s_w_ready")
        s_centred = sem("s_centred")
        s_squared = sem("s_squared")
        s_var = sem("s_var")
        s_sd = sem("s_sd")
        s_h = sem("s_h")
        s_h_table = sem("s_h_table")
        s_counts = sem("s_counts")
        s_totals = sem("s_totals")
        s_tiles_end = sem("s_tiles_end")
        s_end_t = sem("s_end_t")
        s_past_end = sem("s_past_end")
        s_tile_bucket = sem("s_tile_bucket")
        s_cols = sem("s_cols")
        s_cols_staged = sem("s_cols_staged")
        s_code = sem("s_code")
        s_hot_cols = sem("s_hot_cols")
        s_scattered = sem("s_scattered")
        s_lists = sem("s_lists")
        s_acc_clear = sem("s_acc_clear")
        s_staged = sem("s_staged")
        s_gathered = [sem(f"s_gathered{i}") for i in range(RING)]
        s_hot = sem("s_hot")
        s_summed = sem("s_summed")
        s_added = sem("s_added")
        s_neigh = sem("s_neigh")
        s_node_staged = sem("s_node_staged")
        s_node_t = sem("s_node_t")
        s_node_t_in = sem("s_node_t_in")
        s_dense = sem("s_dense")
        s_x1 = sem("s_x1")
        s_kv = sem("s_kv")
        s_q = sem("s_q")
        s_kv_table = [sem(f"s_kv_table{i}") for i in range(2)]
        s_hot_t = sem("s_hot_t")
        s_hot_t_in = sem("s_hot_t_in")
        s_q_edge = sem("s_q_edge")
        s_clipped = sem("s_clipped")
        s_exp = sem("s_exp")
        s_weighted = sem("s_weighted")
        s_out_ready = sem("s_out_ready")
        s_out = sem("s_out")

        block = ctx.enter_context(nc.Block())

        def wait(eng, semaphore, value):
            if not isinstance(value, int) or value > 0:
                eng.wait_ge(semaphore, value)

        def rounds(eng, count, unroll, step):
            for n in range(unroll):
                step(n, n)
            with eng.Fori(1, count // unroll) as i:
                for u in range(unroll):
                    step(i * unroll + u, u)

        DST, SRC = 0, 1
        HOT_BEFORE = [0, GROUPS]
        bank = lambda ps, k: ps[:, k * HALF:(k + 1) * HALF]

        @block.sync
        def _(sp):
            full = (BLK - 1) * P * P
            rows = (N_EDGES - full) // P
            rest = N_EDGES - full - rows * P
            sp.wait_ge(s_raw_set, 1)
            for k, e in enumerate((src, dst)):
                sp.dma_start(raw[:, k, 0:BLK - 1, :], e[0:full].rearrange("(b p e) -> p b e", p=P, e=P)).then_inc(s_edges_in, 16)
                sp.dma_start(raw[0:rows, k, BLK - 1, :], e[full:full + rows * P].rearrange("(p e) -> p e", e=P)).then_inc(s_edges_in, 16)
                sp.dma_start(raw[rows:rows + 1, k, BLK - 1, 0:rest], e[full + rows * P:N_EDGES].rearrange("(p e) -> p e", p=1)).then_inc(s_edges_in, 16)
            sp.wait_ge(s_x_set, 1)
            sp.dma_start(xs[:, 0:NB - 1, :], x[0:(NB - 1) * P, :].rearrange("(t p) f -> p t f", p=P)).then_inc(s_x_in, 16)
            sp.dma_start(xs[0:TAIL, NB - 1, :], x[(NB - 1) * P:N_NODES, :]).then_inc(s_x_in, 16)
            sp.dma_start(w_rows[:, 0, :], w_self).then_inc(s_w_in, 16)
            sp.dma_start(w_rows[:, 1, :], w_neigh).then_inc(s_w_in, 16)
            for k, w in enumerate((qw, kw, vw)):
                sp.dma_start(w_qkv[:, k * D:(k + 1) * D], w).then_inc(s_w_in, 16)
            sp.wait_ge(s_h, 1)
            sp.dma_start(h_table.rearrange("(t p) f -> p t f", p=P), h[:, :, :]).then_inc(s_h_table, 16)
            for i in range(STEPS7):
                sp.wait_ge(s_kv, i + 1)
                sp.dma_start(kv_table[i * NT7 * P:(i + 1) * NT7 * P, :].rearrange("(t p) f -> p t f", p=P), kv_stage[:, i % 2, :, :]).then_inc(s_kv_table[i % 2], 16)
            sp.wait_ge(s_out_ready, 1)
            sp.dma_start(out[0:(NB - 1) * P, :].rearrange("(t p) f -> p t f", p=P), work[:, 0:NB - 1, :]).then_inc(s_out, 16)
            sp.dma_start(out[(NB - 1) * P:N_NODES, :], work[0:TAIL, NB - 1, :]).then_inc(s_out, 16)
            sp.wait_ge(s_h_table, 16)
            for j in range(2):
                sp.wait_ge(s_kv_table[j], 16 * len(range(j, STEPS7, 2)))
            sp.wait_ge(s_out, 32)

        @block.gpsimd
        def _(pool):
            nc.gpsimd.iota(iota_part_i[:, :], [[0, 1]], base=0, channel_multiplier=1).then_inc(s_iota, 1)
            nc.gpsimd.iota(iota_i[:, :], [[1, TILES]], base=0, channel_multiplier=0).then_inc(s_iota, 1)

            def gather_group(table, width, u):
                for g in range(GT):
                    nc.gpsimd.indirect_dma_start(
                        msg[:, u, g, 0:width], None, table,
                        bass.IndirectOffsetOnAxis(ap=idx_stage[:, u, g:g + 1], axis=0)).then_inc(s_gathered[u], 16)

            staged = pool.alloc_register("staged_goal")

            def gather_all(layer, table, width):
                pool.reg_mov(staged, layer * GROUPS + 1)
                with pool.Fori(0, GROUPS // RING) as _i:
                    for u in range(RING):
                        pool.wait_ge(s_staged, staged)
                        pool.reg_add(staged, staged, 1)
                        gather_group(table, width, u)

            pool.wait_ge(s_h_table, 16)
            gather_all(0, h_table, D)
            for j in range(2):
                pool.wait_ge(s_kv_table[j], 16 * len(range(j, STEPS7, 2)))
            gather_all(1, kv_table, 2 * D)

        @block.scalar
        def _(act):
            copy = lambda o, i: nc.scalar.activation(o, i, ACT.Copy)

            def layer_norm_part(k):
                act.wait_ge(s_centred, k + 1)
                nc.scalar.activation(h[:, :, :], work[:, :, :], ACT.Square).then_inc(s_squared, 1)
                act.wait_ge(s_var, k + 1)
                nc.scalar.activation(stat2[:, :], stat[:, :], ACT.Sqrt, bias=eps_col[:, :], scale=1.0 / D).then_inc(s_sd, 1)

            def bucketing_part(k):
                act.wait_ge(s_cols, k + 1)

                def stage_cols(m, u):
                    wait(act, s_hot_cols, k * CHUNKS + m - RING + 1)
                    nc.scalar.copy(cols_stage[:, u, :, :], cols[:, bass.ds(m * GT, GT), :]).then_inc(s_cols_staged, 1)
                rounds(act, CHUNKS, RING, stage_cols)

            def stage_lists(layer, n, u):
                nc.scalar.copy(loc_stage[:, u, :], local[:, bass.ds(n * GT, GT)])
                nc.scalar.copy(idx_stage[:, u, :], other_idx[:, bass.ds(n * GT, GT)]).then_inc(s_staged, 1)

            act.wait_ge(s_x_in, 32)
            act.wait_ge(s_const, 1)
            layer_norm_part(0)
            bucketing_part(DST)
            act.wait_ge(s_lists, 1)

            def stage_group_0(n, u):
                wait(act, s_summed, n - RING + 1)
                stage_lists(0, n, u)
            rounds(act, GROUPS, RING, stage_group_0)

            act.wait_ge(s_neigh, 1)

            for i in range(STEPS7):
                wait(act, s_node_t, i)
                nc.scalar.copy(node_stage[:, 0, :, :], h[:, i * NT7:(i + 1) * NT7, :])
                nc.scalar.copy(node_stage[:, 1, :, :], work[:, i * NT7:(i + 1) * NT7, :]).then_inc(s_node_staged, 1)
                act.wait_ge(s_node_t, i + 1)
                wait(act, s_dense, i)
                copy(node_t[:, 0, :, :], psA[0:D, 0:NT7 * P].rearrange("p (t e) -> p t e", t=NT7)).then_inc(s_node_t_in, 1)
            act.wait_ge(s_x1, STEPS7)
            layer_norm_part(1)
            act.wait_ge(s_h, 2)
            for i in range(STEPS7):
                wait(act, s_node_t, STEPS7 + i)
                nc.scalar.copy(node_stage[:, 0, :, :], h[:, i * NT7:(i + 1) * NT7, :]).then_inc(s_node_staged, 1)
                act.wait_ge(s_node_t, STEPS7 + i + 1)
                wait(act, s_dense, STEPS7 + i)
                copy(node_t[:, 0, :, :], psA[0:D, 0:NT7 * P].rearrange("p (t e) -> p t e", t=NT7)).then_inc(s_node_t_in, 1)
            bucketing_part(SRC)
            act.wait_ge(s_lists, 2)

            for n in range(RING):
                stage_lists(1, n, n)

            def attend_group(n, u, more=True):
                if more:
                    act.wait_ge(s_hot_t, n + 2)
                    wait(act, s_q_edge, n)
                    nc.scalar.copy(hot_t[:, (u + 1) % 2, :, :],
                                   bank(psA, (u + 1) % 2).rearrange("p (g e) -> p g e", g=GT)).then_inc(s_hot_t_in, 1)
                act.wait_ge(s_clipped, n + 1)
                wait(act, s_summed, GROUPS + n - 1)
                nc.scalar.activation(weighted[:, u % 2, :, D:W1],
                                     score[:, u % 2, :].rearrange("p (g h) -> p g h", g=GT), ACT.Exp).then_inc(s_exp, 1)

            act.wait_ge(s_hot_t, 1)
            nc.scalar.copy(hot_t[:, 0, :, :], bank(psA, 0).rearrange("p (g e) -> p g e", g=GT)).then_inc(s_hot_t_in, 1)

            def restage(n, u):
                act.wait_ge(s_weighted, n + 1)
                act.wait_ge(s_hot, GROUPS + n + 1)
                stage_lists(1, n + RING, u)

            for n in range(RING):
                attend_group(n, n)
                restage(n, n)
            with act.Fori(1, GROUPS // RING - 1) as i:
                for u in range(RING):
                    attend_group(i * RING + u, u)
                    restage(i * RING + u, u)
            for u in range(RING):
                attend_group(GROUPS - RING + u, u, more=u < RING - 1)

        @block.vector
        def _(dve):
            chain = [0]

            def link(ins):
                chain[0] = chain[0] + 1
                ins.then_inc(s_dve, 1)
                dve.wait_ge(s_dve, chain[0])

            V = nc.vector
            V.memset(raw[:, :, BLK - 1, :], -1).then_inc(s_raw_set, 1)
            V.memset(xs[:, NB - 1, :], 0.0).then_inc(s_x_set, 1)
            V.memset(ones[:, :], 1.0)
            V.memset(ones_row[:, :], 1.0)
            V.memset(ones_h[:, :], 1.0)
            V.memset(zeros_h[:, :], 0.0)
            V.memset(eps_col[:, :], EPS_LN)
            V.memset(msg[:, :, :, D:W0], 1.0)
            dve.wait_ge(s_iota, 2)
            link(V.tensor_copy(iota_part[:, :], iota_part_i[:, :]))
            link(V.tensor_copy(iota_f[:, :], iota_i[:, 0:P]))
            V.tensor_copy(iota_h[:, :], iota_i[:, :])
            V.tensor_scalar(before[:, :], iota_f[:, :], iota_part[:, :], None, ALU.is_gt)
            V.tensor_scalar(ident[:, :], iota_f[:, :], iota_part[:, :], None, ALU.is_equal).then_inc(s_const, 1)

            dve.wait_ge(s_edges_in, 96)
            V.tensor_copy(raw_f[:, :, :, :], raw[:, :, :, :]).then_inc(s_raw_f, 1)
            for k in range(2):
                dve.wait_ge(s_edge_t, k + 1)
                V.tensor_copy(edge[k][:, :], psB[:, 0:BLK * P] if k == 0 else psC[:, 0:BLK * P]).then_inc(s_edge, 1)
            dve.wait_ge(s_w_t, 1)
            V.tensor_copy(w_in[:, :, :], psD[0:D, 0:2 * D].rearrange("p (w f) -> p w f", w=2)).then_inc(s_w_ready, 1)
            dve.wait_ge(s_w_ready, 1)
            dve.wait_ge(s_edge, 2)

            bc = lambda ap, n: ap.unsqueeze(2).to_broadcast([P, NB, n])

            def layer_norm(k, source):
                link(V.tensor_reduce(stat[:, :], source[:, :, :], X, ALU.add))
                link(V.tensor_scalar(stat[:, :], stat[:, :], 1.0 / D, None, ALU.mult))
                V.tensor_tensor(work[:, :, :], source[:, :, :], bc(stat[:, :], D), ALU.subtract).then_inc(s_centred, 1)
                dve.wait_ge(s_squared, k + 1)
                V.tensor_reduce(stat[:, :], h[:, :, :], X, ALU.add).then_inc(s_var, 1)
                dve.wait_ge(s_sd, k + 1)
                link(V.reciprocal(stat[:, :], stat2[:, :]))
                link(V.tensor_tensor(work[:, :, :], work[:, :, :], bc(stat[:, :], D), ALU.mult))
                V.tensor_scalar(h[:, :, :], work[:, :, :], 0.0, None, ALU.max).then_inc(s_h, 1)
                dve.wait_ge(s_h, k + 1)

            def bucket_edges(k, key, other):
                keys, others = key[:, 0:RAWT], other[:, 0:RAWT]
                link(V.tensor_copy(ints[:, 0:RAWT], keys))
                link(V.tensor_scalar(ints[:, 0:RAWT], ints[:, 0:RAWT], 7, None, ALU.arith_shift_right))
                link(V.tensor_copy(bucket[:, :], ints[:, 0:RAWT]))
                link(V.tensor_copy(ints[:, 0:RAWT], others))
                link(V.tensor_scalar(ints[:, 0:RAWT], ints[:, 0:RAWT], 10, None, ALU.arith_shift_right))
                link(V.tensor_copy(mask[:, :], ints[:, 0:RAWT]))
                link(V.scalar_tensor_tensor(scan[:, 0:RAWT], mask[:, :], -1024.0, others, ALU.mult, ALU.add))
                link(V.tensor_scalar(cols[:, :, 3], scan[:, 0:RAWT], 1.0 / 1024.0, None, ALU.mult))
                link(V.scalar_tensor_tensor(scan[:, 0:RAWT], bucket[:, :], -128.0, keys, ALU.mult, ALU.add))
                link(V.tensor_scalar(scan[:, 0:RAWT], scan[:, 0:RAWT], 1.0, 8.0, ALU.add, ALU.mult))
                link(V.tensor_tensor(cols[:, :, 2], scan[:, 0:RAWT], mask[:, :], ALU.add))
                start = chain[0]
                with dve.Fori(0, NB) as b:
                    chain[0] = b * 1 + start
                    link(V.tensor_scalar(mask[:, :], bucket[:, :], iota_f[:, bass.ds(b, 1)], None, ALU.is_equal, ALU.add,
                                         accum_out=counts[:, bass.ds(b, 1)]))
                chain[0] = start + NB
                link(V.memset(position[:, :], 0.0))
                V.tensor_copy(tiles_f[:, :], counts[:, :]).then_inc(s_counts, 1)
                dve.wait_ge(s_totals, k + 1)
                link(V.tensor_scalar(tiles_i[:, :], psB[:, NB:2 * NB], P - 1.0, None, ALU.add))
                link(V.tensor_scalar(tiles_i[:, :], tiles_i[:, :], 7, None, ALU.arith_shift_right))
                link(V.tensor_copy(tiles_f[:, :], tiles_i[:, :]))
                V.tensor_tensor_scan(tiles_end[:, :], ones[:, 0:NB], tiles_f[:, :], 0.0, ALU.mult, ALU.add).then_inc(s_tiles_end, 1)
                dve.wait_ge(s_tiles_end, k + 1)
                link(V.tensor_tensor(base[:, :], tiles_end[:, :], tiles_f[:, :], ALU.subtract))
                link(V.scalar_tensor_tensor(base[:, :], base[:, :], float(P), psB[:, 0:NB], ALU.mult, ALU.add))
                dve.wait_ge(s_end_t, k + 1)
                link(V.tensor_copy(end_col[0:NB, :], psD[0:NB, 0:1]))
                V.tensor_scalar(past_end[0:NB, :], iota_h[0:NB, :], end_col[0:NB, :], None, ALU.is_ge).then_inc(s_past_end, 1)
                dve.wait_ge(s_tile_bucket, k + 1)
                V.tensor_scalar(tile_bucket[:, :], psC[0:1, 0:TILES], NB - 1.0, None, ALU.min)
                start = chain[0]
                with dve.Fori(0, NB) as b:
                    chain[0] = b * 4 + start
                    link(V.tensor_scalar(mask[:, :], bucket[:, :], iota_f[:, bass.ds(b, 1)], None, ALU.is_equal))
                    link(V.tensor_tensor_scan(scan[:, 0:RAWT], ones_row[:, :], mask[:, :], base[:, bass.ds(b, 1)], ALU.mult, ALU.add))
                    link(V.tensor_tensor(scan[:, 0:RAWT], scan[:, 0:RAWT], mask[:, :], ALU.mult))
                    link(V.tensor_tensor(position[:, :], position[:, :], scan[:, 0:RAWT], ALU.add))
                chain[0] = start + 4 * NB
                link(V.tensor_scalar(position[:, :], position[:, :], -1.0, None, ALU.add))
                link(V.tensor_copy(ints[:, 0:RAWT], position[:, :]))
                link(V.tensor_scalar(ints[:, 0:RAWT], ints[:, 0:RAWT], 7, None, ALU.arith_shift_right))
                link(V.tensor_copy(cols[:, :, 1], ints[:, 0:RAWT]))
                V.scalar_tensor_tensor(cols[:, :, 0], cols[:, :, 1], -128.0, position[:, :], ALU.mult, ALU.add).then_inc(s_cols, 1)

                def scatter_chunk(m, u):
                    dve.wait_ge(s_cols_staged, k * CHUNKS + 1 + m)
                    wait(dve, s_scattered, k * CHUNKS + m - 1)
                    for g in range(GT):
                        c = lambda j: cols_stage[:, u, g, j:j + 1]
                        V.tensor_scalar(hot_tile[:, u % 2, g, :], iota_h[:, :], c(1), None, ALU.is_equal)
                        V.tensor_scalar(hot_row[:, u % 2, g, 0, :], iota_h[:, 0:P], c(0), c(2), ALU.is_equal, ALU.mult)
                        last = V.tensor_scalar(hot_row[:, u % 2, g, 1, :], iota_h[:, 0:P], c(0), c(3), ALU.is_equal, ALU.mult)
                    last.then_inc(s_hot_cols, 1)
                rounds(dve, CHUNKS, RING, scatter_chunk)
                dve.wait_ge(s_code, k + 1)
                code = scan[:, :].bitcast(i32)
                link(V.tensor_scalar(code, psA[:, 0:TILES], 1024.0, None, ALU.mult))
                link(V.tensor_scalar(ints[:, :], code, 13, None, ALU.arith_shift_right))
                link(V.tensor_scalar(other_idx[:, :], code, 8191, None, ALU.bitwise_and))
                V.tensor_scalar(local[:, :], ints[:, :], -1.0, None, ALU.add).then_inc(s_lists, 1)

            def make_hot(layer, n, u):
                dve.wait_ge(s_staged, layer * GROUPS + 1 + n)
                for g in range(GT):
                    last = V.tensor_scalar(hot[:, u, g, :], iota_f[:, :], loc_stage[:, u, g:g + 1], None, ALU.is_equal)
                last.then_inc(s_hot, 1)

            bucket_regs = [dve.alloc_register(f"bucket{g}") for g in range(GT)]

            def add_group(layer, n, u, width, ps):
                for g in range(GT):
                    dve.reg_load(bucket_regs[g], tile_bucket[0:1, bass.ds(n * GT + g, 1)])
                dve.wait_ge(s_summed, layer * GROUPS + 1 + n)
                for g in range(GT):
                    b = dve.snap(bucket_regs[g], min_val=0, max_val=NB - 1)
                    sums = acc[:, bass.ds(b, 1), 0:width].rearrange("p a f -> p (a f)")
                    V.tensor_tensor(sums, sums, bank(ps, u % 2)[:, g * W1:g * W1 + width], ALU.add).then_inc(s_added, 1)
                    dve.wait_ge(s_added, layer * TILES + 1 + g + n * GT)

            dve.wait_ge(s_x_in, 32)
            layer_norm(0, xs)
            bucket_edges(DST, edge[1], edge[0])
            link(V.memset(acc[:, :, :], 0.0))
            dve.wait_ge(s_lists, 1)

            def sum_step(n, u):
                make_hot(0, n, u)
                add_group(0, n, u, W0, psB)
            rounds(dve, GROUPS, RING, sum_step)

            deg = acc[:, :, D:W0].rearrange("p t o -> p (t o)")
            link(V.tensor_scalar(stat[:, :], deg, EPS, None, ALU.add))
            link(V.reciprocal(stat[:, :], stat[:, :]))
            link(V.tensor_scalar(work[:, :, :], acc[:, :, 0:D], EPS, None, ALU.add))
            V.tensor_tensor(work[:, :, :], work[:, :, :], bc(stat[:, :], D), ALU.mult).then_inc(s_neigh, 1)
            PER = HALF // D
            for i in range(STEPS7):
                dve.wait_ge(s_node_t, i + 1)
                wait(dve, s_dense, i)
                V.tensor_copy(node_t[:, 1, :, :], psB[0:D, 0:NT7 * P].rearrange("p (t e) -> p t e", t=NT7)).then_inc(s_node_t_in, 1)
                dve.wait_ge(s_dense, i + 1)
                for k, (a, b) in enumerate(((0, PER), (PER, NT7))):
                    xt = xs[:, i * NT7 + a:i * NT7 + b, :]
                    last = V.tensor_tensor(xt, xt, bank(psC, k)[:, 0:(b - a) * D].rearrange("p (t f) -> p t f", f=D), ALU.add)
                last.then_inc(s_x1, 1)
            dve.wait_ge(s_x1, STEPS7)
            layer_norm(1, xs)
            for i in range(STEPS7):
                dve.wait_ge(s_dense, STEPS7 + i + 1)
                if i >= 2:
                    dve.wait_ge(s_kv_table[i % 2], 16 * (i // 2))
                for k, (a, b) in enumerate(((0, PER), (PER, NT7))):
                    V.tensor_copy(q[:, i * NT7 + a:i * NT7 + b, :], bank(psB, k)[:, 0:(b - a) * D].rearrange("p (t f) -> p t f", f=D))
                for k in range(4):
                    a, b = 2 * k, min(2 * k + 2, NT7)
                    last = V.tensor_copy(kv_stage[:, i % 2, a:b, :], bank(psC if k < 2 else psD, k % 2)[:, 0:(b - a) * 2 * D].rearrange("p (t f) -> p t f", f=2 * D))
                last.then_inc(s_kv, 1)
            dve.wait_ge(s_kv, STEPS7)
            bucket_edges(SRC, edge[0], edge[1])
            link(V.memset(acc[:, :, :], 0.0))
            dve.wait_ge(s_lists, 2)
            make_hot(1, 0, 0)

            steps = [0]

            def attend_step(n, u, first=False, more=True):
                if more:
                    make_hot(1, n + 1, (u + 1) % RING)
                dve.wait_ge(s_q_edge, n + 1)
                dve.wait_ge(s_gathered[u], gathered(n, u))
                start = chain[0]
                link(V.tensor_tensor(prod[:, :, :], bank(psB, u % 2)[:, 0:GT * D].rearrange("p (g f) -> p g f", g=GT),
                                     msg[:, u, :, 0:D], ALU.mult))
                link(V.tensor_reduce(score[:, u % 2, :], prod[:, :, :].rearrange("p g (h d) -> p (g h) d", d=DH), X, ALU.add))
                V.tensor_scalar(score[:, u % 2, :], score[:, u % 2, :], -10.0, 10.0, ALU.max, ALU.min).then_inc(s_clipped, 1)
                if not first:
                    add_group(1, n - 1, u - 1, W1, psC)
                dve.wait_ge(s_exp, n + 1)
                for g in range(GT):
                    e = weighted[:, u % 2, g, D:W1]
                    last = V.tensor_tensor(weighted[:, u % 2, g, 0:D].rearrange("p (h d) -> p h d", h=HEADS),
                                           msg[:, u, g, D:2 * D].rearrange("p (h d) -> p h d", h=HEADS),
                                           e.unsqueeze(2).to_broadcast([P, HEADS, DH]), ALU.mult)
                last.then_inc(s_weighted, 1)

            per_step = 2
            def gathered(n, u):
                return 16 * GT * (GROUPS // RING) + 16 * GT * ((n - u) // RING + 1 if isinstance(n, int) else 0)

            before_loop = chain[0]
            for n in range(RING):
                attend_step(n, n, first=n == 0)
            rounds_in = 16 * GT * (GROUPS // RING)
            with dve.Fori(1, GROUPS // RING - 1) as i:
                gathered = lambda n, u: i * (16 * GT) + (rounds_in + 16 * GT)
                for u in range(RING):
                    chain[0] = i * (per_step * RING) + (before_loop + per_step * u)
                    attend_step(i * RING + u, u)
            chain[0] = before_loop + per_step * (GROUPS - RING)
            gathered = lambda n, u: 2 * rounds_in
            for u in range(RING):
                attend_step(GROUPS - RING + u, u, more=u < RING - 1)
            add_group(1, GROUPS - 1, RING - 1, W1, psC)
            link(V.tensor_scalar(rec[:, :, :], acc[:, :, D:W1], EPS, None, ALU.add))
            link(V.reciprocal(rec[:, :, :], rec[:, :, :]))
            link(V.tensor_tensor(xs[:, :, :], xs[:, :, :], h[:, :, :], ALU.add))
            for hd in range(HEADS):
                V.tensor_tensor(work[:, :, hd * DH:(hd + 1) * DH], acc[:, :, hd * DH:(hd + 1) * DH],
                                rec[:, :, hd:hd + 1].to_broadcast([P, NB, DH]), ALU.mult).then_inc(s_dve, 1)
            chain[0] += HEADS
            dve.wait_ge(s_dve, chain[0])
            V.tensor_tensor(work[:, :, :], work[:, :, :], xs[:, :, :], ALU.add).then_inc(s_out_ready, 1)

        @block.tensor
        def _(pe):
            mm = nc.tensor.matmul
            pe.wait_ge(s_const, 1)
            pe.wait_ge(s_raw_f, 1)
            for k, ps in ((0, psB), (1, psC)):
                for b in range(BLK):
                    last = nc.tensor.transpose(ps[:, b * P:(b + 1) * P], raw_f[:, k, b, :], ident[:, :])
                last.then_inc(s_edge_t, 1)
            pe.wait_ge(s_w_in, 80)
            for k in range(2):
                last = nc.tensor.transpose(psD[0:D, k * D:(k + 1) * D], w_rows[:, k, :], ident[0:D, 0:D])
            last.then_inc(s_w_t, 1)

            def bucketing_part(k):
                pe.wait_ge(s_counts, k + 1)
                pe.wait_ge(s_edge, 2)
                mm(psB[:, 0:NB], before[:, :], counts[:, :], start=True, stop=True)
                mm(psB[:, NB:2 * NB], ones[:, :], counts[:, :], start=True, stop=True).then_inc(s_totals, 1)
                pe.wait_ge(s_tiles_end, k + 1)
                mm(psD[0:NB, 0:1], tiles_end[0:1, :], ones[0:1, 0:1], start=True, stop=True).then_inc(s_end_t, 1)
                pe.wait_ge(s_past_end, k + 1)
                mm(psC[0:1, 0:HALF], ones_h[0:NB, :], past_end[0:NB, 0:HALF], start=True, stop=True)
                mm(psC[0:1, HALF:TILES], ones_h[0:NB, :], past_end[0:NB, HALF:TILES], start=True, stop=True).then_inc(s_tile_bucket, 1)
                wait(pe, s_node_t_in, k * 3 * STEPS7)
                for lo, hi in ((0, HALF), (HALF, TILES)):
                    mm(psA[:, lo:hi], zeros_h[:, :], iota_h[:, lo:hi], start=True, stop=False)

                def scatter_chunk(m, u):
                    pe.wait_ge(s_hot_cols, k * CHUNKS + 1 + m)
                    for g in range(GT):
                        for part in range(2):
                            for lo, hi in ((0, HALF), (HALF, TILES)):
                                last = mm(psA[:, lo:hi], hot_row[:, u % 2, g, part, :], hot_tile[:, u % 2, g, lo:hi],
                                          start=False, stop=False)
                    last.then_inc(s_scattered, 1)
                rounds(pe, CHUNKS, RING, scatter_chunk)
                for lo, hi in ((0, HALF), (HALF, TILES)):
                    last = mm(psA[:, lo:hi], zeros_h[:, :], iota_h[:, lo:hi], start=False, stop=True)
                last.then_inc(s_code, 1)

            bucketing_part(DST)

            def sum_group(n, u):
                pe.wait_ge(s_hot, n + 1)
                pe.wait_ge(s_gathered[u], gathered(n, u))
                wait(pe, s_added, (n - 1) * GT)
                for g in range(GT):
                    last = mm(bank(psB, u % 2)[:, g * W1:g * W1 + W0], hot[:, u, g, :], msg[:, u, g, 0:W0], start=True, stop=True)
                last.then_inc(s_summed, 1)

            gathered = lambda n, u: 16 * GT
            for n in range(RING):
                sum_group(n, n)
            with pe.Fori(1, GROUPS // RING) as i:
                gathered = lambda n, u: i * (16 * GT) + 16 * GT
                for u in range(RING):
                    sum_group(i * RING + u, u)

            pe.wait_ge(s_w_ready, 1)
            PER = HALF // D
            for i in range(STEPS7):
                pe.wait_ge(s_node_staged, i + 1)
                wait(pe, s_node_t_in, 2 * i)
                for k, ps in ((0, psA), (1, psB)):
                    for t in range(NT7):
                        last = nc.tensor.transpose(ps[0:D, t * P:(t + 1) * P], node_stage[:, k, t, :], ident[:, :])
                last.then_inc(s_node_t, 1)
                pe.wait_ge(s_node_t_in, 2 * (i + 1))
                wait(pe, s_x1, i)
                for t in range(NT7):
                    o = bank(psC, t // PER)[:, (t % PER) * D:(t % PER + 1) * D]
                    mm(o, node_t[:, 0, t, :], w_in[:, 0, :], start=True, stop=False)
                    last = mm(o, node_t[:, 1, t, :], w_in[:, 1, :], start=False, stop=True)
                last.then_inc(s_dense, 1)
            for i in range(STEPS7):
                pe.wait_ge(s_node_staged, STEPS7 + i + 1)
                for t in range(NT7):
                    last = nc.tensor.transpose(psA[0:D, t * P:(t + 1) * P], node_stage[:, 0, t, :], ident[:, :])
                last.then_inc(s_node_t, 1)
                pe.wait_ge(s_node_t_in, 2 * STEPS7 + i + 1)
                wait(pe, s_kv, i)
                for t in range(NT7):
                    mm(bank(psB, t // PER)[:, (t % PER) * D:(t % PER + 1) * D], node_t[:, 0, t, :], w_qkv[:, 0:D], start=True, stop=True)
                    last = mm(bank(psC if t < 4 else psD, t // 2 % 2)[:, (t % 2) * 2 * D:(t % 2 + 1) * 2 * D], node_t[:, 0, t, :],
                              w_qkv[:, D:3 * D], start=True, stop=True)
                last.then_inc(s_dense, 1)
            bucketing_part(SRC)

            q_regs = [pe.alloc_register(f"q_bucket{g}") for g in range(GT)]

            def transpose_hot(n, u):
                pe.wait_ge(s_hot, GROUPS + 1 + n)
                wait(pe, s_hot_t_in, n - 1)
                for g in range(GT):
                    last = nc.tensor.transpose(bank(psA, u % 2)[:, g * P:(g + 1) * P], hot[:, u, g, :], ident[:, :])
                last.then_inc(s_hot_t, 1)

            def q_of_edges(n, u):
                for g in range(GT):
                    pe.reg_load(q_regs[g], tile_bucket[0:1, bass.ds(n * GT + g, 1)])
                pe.wait_ge(s_hot_t_in, n + 1)
                wait(pe, s_clipped, n - 1)
                for g in range(GT):
                    b = pe.snap(q_regs[g], min_val=0, max_val=NB - 1)
                    last = mm(bank(psB, u % 2)[:, g * D:(g + 1) * D], hot_t[:, u % 2, g, :],
                              q[:, bass.ds(b, 1), :].rearrange("p a f -> p (a f)"), start=True, stop=True)
                last.then_inc(s_q_edge, 1)

            def sum_weighted(n, u):
                pe.wait_ge(s_weighted, n + 1)
                wait(pe, s_added, n * GT - GT + TILES)
                for g in range(GT):
                    last = mm(bank(psC, u % 2)[:, g * W1:(g + 1) * W1], hot[:, u, g, :], weighted[:, u % 2, g, :], start=True, stop=True)
                last.then_inc(s_summed, 1)

            pe.wait_ge(s_lists, 2)
            transpose_hot(0, 0)
            q_of_edges(0, 0)

            def attend_step(n, u, more=True):
                if more:
                    transpose_hot(n + 1, (u + 1) % RING)
                    q_of_edges(n + 1, (u + 1) % RING)
                sum_weighted(n, u)
            for n in range(RING):
                attend_step(n, n)
            with pe.Fori(1, GROUPS // RING - 1) as i:
                for u in range(RING):
                    attend_step(i * RING + u, u)
            for u in range(RING):
                attend_step(GROUPS - RING + u, u, more=u < RING - 1)


def kernel(x, src, dst, L0_gnn_W_self, L0_gnn_W_neigh, L1_gnn_qW, L1_gnn_kW, L1_gnn_vW):
    import numpy as np
    import concourse.bacc as bacc
    from concourse.bass_utils import run_bass_kernel_spmd

    nc = bacc.Bacc("TRN2", target_bir_lowering=False, num_devices=1)
    given = dict(x=x, src=src, dst=dst, w_self=L0_gnn_W_self, w_neigh=L0_gnn_W_neigh, qw=L1_gnn_qW, kw=L1_gnn_kW, vw=L1_gnn_vW)
    arrays, args = {}, []
    for name, a in given.items():
        a = np.ascontiguousarray(a)
        arrays["in_" + name] = a
        args.append(nc.dram_tensor("in_" + name, a.shape, mybir.dt.from_np(a.dtype), kind="ExternalInput").ap())
    h_table = nc.dram_tensor("h_table", (NPAD, D), mybir.dt.float32, kind="Internal").ap()
    kv_table = nc.dram_tensor("kv_table", (NPAD, 2 * D), mybir.dt.float32, kind="Internal").ap()
    out = nc.dram_tensor("out", (N_NODES, D), mybir.dt.float32, kind="ExternalOutput").ap()
    gnn_program(nc, *args, h_table, kv_table, out)
    r = run_bass_kernel_spmd(nc, [arrays], core_ids=[0])
    return r.results[0]["out"]
```

```python
import concourse.bass as bass
from concourse import mybir
from contextlib import ExitStack

P = 128
N_NODES = 6250
N_EDGES = 100000
D = 96
HEADS = 4
DH = D // HEADS
EPS_LN = 1e-5
EPS = 1e-8
NB = -(-N_NODES // P)
NPAD = NB * P
TAIL = N_NODES - (NB - 1) * P
BLK = -(-(-(-N_EDGES // P)) // P)
GT = 4
RAWT = -(-(-(-N_EDGES // P)) // GT) * GT
RAW_GROUPS = RAWT // GT
RING = 4
CC = 3
GROUPS0 = -(-((N_EDGES + NB * (GT * P - 1)) // (GT * P)) // RING) * RING
TILES0 = GROUPS0 * GT
TILES1 = -(-((N_EDGES + NB * (P - 1)) // P) // (GT * RING)) * GT * RING
GROUPS1 = TILES1 // GT
AHEAD = RING * GT
NEXT = 64
A_COUNTS = 3
A_GROUPS = (NB - 1) // A_COUNTS
B_GROUPS = NB - 1
C_GROUPS = RAW_GROUPS - A_GROUPS - B_GROUPS
C_CHUNKS = -(-(-(-RAWT // CC)) // C_GROUPS)
CHUNKS = C_CHUNKS * C_GROUPS
COLS = CHUNKS * CC
assert CHUNKS % 4 == 0 and C_CHUNKS == 2 and A_GROUPS * A_COUNTS == NB - 1
assert A_GROUPS % RING == B_GROUPS % RING == C_GROUPS % RING == 0 and COLS <= BLK * P
W0 = D + 1
SPLIT = 3 * D + 2
MID, LOW = D + 1, 2 * D + 1
W1 = D + HEADS
NT7 = 7
STEPS7 = NB // NT7
HALF = 512
assert NB <= NEXT and GT * 6 <= 24 and NB % NT7 == 0 and max(TILES0, TILES1) <= 2 * HALF


class Bucketing:

    def __init__(self, name, sem, key, other, unit_shift, units, lists, unit_bucket):
        self.key, self.other = key, other
        self.unit_shift, self.units, self.tiles = unit_shift, units, (units << unit_shift) // P
        self.other_idx, self.local = lists
        self.unit_bucket = unit_bucket
        self.step = sem(f"s_{name}_step")
        self.counts = sem(f"s_{name}_counts")
        self.totals = sem(f"s_{name}_totals")
        self.units_end = sem(f"s_{name}_units_end")
        self.end_t = sem(f"s_{name}_end_t")
        self.past_end = sem(f"s_{name}_past_end")
        self.unit_bucket_sum = sem(f"s_{name}_unit_bucket_sum")
        self.cols = sem(f"s_{name}_cols")
        self.cols_staged = sem(f"s_{name}_cols_staged")
        self.hot_rows = sem(f"s_{name}_hot_rows")
        self.hot_tiles = sem(f"s_{name}_hot_tiles")
        self.code_rows = sem(f"s_{name}_code_rows")
        self.scattered = sem(f"s_{name}_scattered")
        self.code = sem(f"s_{name}_code")
        self.lists = sem(f"s_{name}_lists")


def gnn_program(nc, x, src, dst, w_self, w_neigh, qw, kw, vw, h_table, kv_table, out):
    f32, i32, f16, bf16 = mybir.dt.float32, mybir.dt.int32, mybir.dt.float16, mybir.dt.bfloat16
    ALU = mybir.AluOpType
    ACT = mybir.ActivationFunctionType
    X = mybir.AxisListType.X

    with ExitStack() as ctx:
        def sb(name, shape, dt):
            return ctx.enter_context(nc.sbuf_tensor(name, shape, dt))

        def sem(name):
            return ctx.enter_context(nc.semaphore(name))

        iota_h = sb("iota_h", [P, TILES0], f16)
        iota_f = sb("iota_f", [P, P], f32)
        iota_b = sb("iota_b", [P, 2 * P], bf16)
        iota_part_i = sb("iota_part_i", [P, 1], i32)
        iota_part = sb("iota_part", [P, 1], f32)
        ident = sb("ident", [P, P], f32)
        before = sb("before", [P, P], f32)
        ones = sb("ones", [P, P], f32)
        ones_h = sb("ones_h", [P, 1], f16)
        zeros_h = sb("zeros_h", [P, P], f16)
        eps_col = sb("eps_col", [P, 1], f32)
        w_rows = sb("w_rows", [D, 2, D], f32)
        w_in = sb("w_in", [D, 2, D], f32)
        w_qkv = sb("w_qkv", [D, 3 * D], f32)
        edge_src = sb("edge_src", [P, BLK * P], f32)
        edge_dst = sb("edge_dst", [P, BLK * P], f32)
        mask = sb("mask", [P, COLS], f16)
        scan = sb("scan", [P, TILES0], f32)
        position = sb("position", [P, COLS], f32)
        counts = sb("counts", [P, NB], f32)
        units_i = sb("units_i", [P, NB], i32)
        units_f = sb("units_f", [P, NB], f32)
        units_end = sb("units_end", [P, NB], f32)
        base = sb("base", [P, NB], f32)
        end_col = sb("end_col", [P, 1], f32)
        cols_stage = sb("cols_stage", [P, 4, CC, 4], f32)
        hot_tile = sb("hot_tile", [P, 2, CC, TILES0], f16)
        hot_row = sb("hot_row", [P, 2, CC, P], f16)
        code_row = sb("code_row", [P, 2, CC, 2, P], f16)
        idx0 = sb("idx0", [P, TILES0 + AHEAD], i32)
        local0 = sb("local0", [P, TILES0 + AHEAD], f32)
        idx1 = sb("idx1", [P, TILES1 + AHEAD], i32)
        local1 = sb("local1", [P, TILES1 + AHEAD], f32)
        window = sb("window", [1, 2, 2 * P], i32)
        bucket1 = sb("bucket1", [1, TILES1], i32)
        packed1 = sb("packed1", [1, GROUPS1 + RING], i32)
        slow = sb("slow", [1, 1], i32)
        xs = sb("xs", [P, NB, D], f32)
        h = sb("h", [P, NB, D], f32)
        work = sb("work", [P, NB, D], f32)
        parts = sb("parts", [P, NB, SPLIT], bf16)
        stat = sb("stat", [P, NB], f32)
        stat2 = sb("stat2", [P, NB], f32)
        acc = sb("acc", [P, NB + 1, W1], f32)
        rec = sb("rec", [P, NB, HEADS], f32)
        idx_stage = sb("idx_stage", [P, RING, GT], i32)
        loc_stage = sb("loc_stage", [P, RING, GT], f32)
        msg = sb("msg", [P, RING, GT, 2 * D], f32)
        hot = sb("hot", [P, RING, GT, P], f32)
        hot_t = sb("hot_t", [P, 2, GT, P], bf16)
        prod = sb("prod", [P, GT, D], f32)
        score = sb("score", [P, 2, GT * HEADS], f32)
        weighted = sb("weighted", [P, 2, GT, W1], f32)
        node_t = sb("node_t", [D, 2, NT7, P], f32)

        flat = lambda t: t.rearrange("p a f -> p (a f)")
        flat3 = lambda t: t.rearrange("p a b f -> p (a b f)")
        raw = flat3(hot[:, :, :, :])[:, 0:2 * BLK * P].bitcast(i32).rearrange("p (k b e) -> p k b e", k=2, b=BLK)
        raw_f = flat3(msg[:, :, :, :])[:, 0:2 * BLK * P].rearrange("p (k b e) -> p k b e", k=2, b=BLK)
        iota_i = flat3(msg[:, :, :, :])[:, 2 * BLK * P:2 * BLK * P + TILES0].bitcast(i32)
        msg0 = flat3(msg[:, :, :, :])[:, 0:RING * GT * SPLIT // 2].bitcast(bf16).rearrange("p (r g f) -> p r g f", r=RING, g=GT)
        hot0 = flat3(hot[:, :, :, :]).bitcast(bf16).rearrange("p (r g e) -> p r g e", r=RING, g=GT)
        node_stage = flat3(hot[:, :, :, :])[:, 0:2 * NT7 * D].rearrange("p (k t f) -> p k t f", k=2, t=NT7)
        kv_stage = flat3(msg[:, :, :, :])[:, 0:4 * NT7 * D].rearrange("p (k t f) -> p k t f", k=2, t=NT7)
        CPAD = COLS + 2 * CC
        cols = flat(work[:, :, :])[:, 0:4 * CPAD].rearrange("p (t c) -> p t c", c=4)
        ints = flat(work[:, :, :])[:, 4 * CPAD:4 * CPAD + TILES0].bitcast(i32)
        bucket = flat(work[:, :, :])[:, 4 * CPAD + TILES0:4 * CPAD + TILES0 + COLS // 2].bitcast(f16)
        past_end = hot_tile[:, 0, 0, :]
        g_span = units_f[0:BLK, 0:1]

        psA = ctx.enter_context(nc.psum_tensor("psA", [P, 2 * HALF], f32))
        psB = ctx.enter_context(nc.psum_tensor("psB", [P, 2 * HALF], f32))
        psC = ctx.enter_context(nc.psum_tensor("psC", [P, 2 * HALF], f32))
        psD = ctx.enter_context(nc.psum_tensor("psD", [P, 2 * HALF], f32))

        BK0 = Bucketing("bk0", sem, edge_dst, edge_src, 9, GROUPS0, (idx0, local0), window[:, 0, :])
        BK1 = Bucketing("bk1", sem, edge_src, edge_dst, 7, TILES1, (idx1, local1), bucket1[:, :])

        s_raw_set = sem("s_raw_set")
        s_edges_in = sem("s_edges_in")
        s_x_set = sem("s_x_set")
        s_x_in = sem("s_x_in")
        s_w_in = sem("s_w_in")
        s_iota = sem("s_iota")
        s_const = sem("s_const")
        s_dve = sem("s_dve")
        s_raw_f = sem("s_raw_f")
        s_edge_t = sem("s_edge_t")
        s_edge = sem("s_edge")
        s_w_t = sem("s_w_t")
        s_w_ready = sem("s_w_ready")
        s_centred = sem("s_centred")
        s_squared = sem("s_squared")
        s_var = sem("s_var")
        s_sd = sem("s_sd")
        s_h = sem("s_h")
        s_parts = sem("s_parts")
        s_h_table = sem("s_h_table")
        s_tile_ends = sem("s_tile_ends")
        s_tile_ends_t = sem("s_tile_ends_t")
        s_windows = sem("s_windows")
        s_window_row = sem("s_window_row")
        s_window_f = sem("s_window_f")
        s_window_all = sem("s_window_all")
        s_wide = sem("s_wide")
        s_lists0 = sem("s_lists0")
        s_staged0 = sem("s_staged0")
        s_gathered0 = [sem(f"s_gathered0_{i}") for i in range(RING)]
        s_gathered1 = [sem(f"s_gathered1_{i}") for i in range(RING)]
        s_hot0 = sem("s_hot0")
        s_summed0 = sem("s_summed0")
        s_added0 = sem("s_added0")
        s_neigh = sem("s_neigh")
        s_node_staged = sem("s_node_staged")
        s_node_t = sem("s_node_t")
        s_node_t_in = sem("s_node_t_in")
        s_dense = sem("s_dense")
        s_x1 = sem("s_x1")
        s_kv = sem("s_kv")
        s_q = sem("s_q")
        s_kv_table = [sem(f"s_kv_table{i}") for i in range(2)]
        s_staged1 = sem("s_staged1")
        s_hot1 = sem("s_hot1")
        s_hot_t = sem("s_hot_t")
        s_hot_t_in = sem("s_hot_t_in")
        s_q_edge = sem("s_q_edge")
        s_clipped = sem("s_clipped")
        s_exp = sem("s_exp")
        s_weighted = sem("s_weighted")
        s_summed1 = sem("s_summed1")
        s_added1 = sem("s_added1")
        s_out_ready = sem("s_out_ready")
        s_out = sem("s_out")

        block = ctx.enter_context(nc.Block())

        def wait(eng, semaphore, value):
            if not isinstance(value, int) or value > 0:
                eng.wait_ge(semaphore, value)

        def rounds(eng, count, step):
            for n in range(RING):
                step(n, n)
            with eng.Fori(1, count // RING) as i:
                for u in range(RING):
                    step(i * RING + u, u)

        def is_slow(eng, name):
            eng.wait_ge(s_wide, 1)
            r = eng.alloc_register(name)
            eng.reg_load(r, slow[0:1, 0:1])
            return r

        def unpack(eng, regs, packed):
            for g, reg in enumerate(regs):
                if g:
                    eng.reg_alu(reg, packed, 6 * g, ALU.logical_shift_right)
                eng.reg_alu(reg, reg if g else packed, NEXT - 1, ALU.bitwise_and)

        bank = lambda ps, k: ps[:, k * HALF:(k + 1) * HALF]
        halves = lambda n: ((0, HALF), (HALF, n)) if n > HALF else ((0, n),)
        PER = HALF // D
        A, B, C = A_GROUPS, A_GROUPS + B_GROUPS, RAW_GROUPS

        @block.sync
        def _(sp):
            full = (BLK - 1) * P * P
            rows = (N_EDGES - full) // P
            rest = N_EDGES - full - rows * P
            sp.wait_ge(s_x_set, 1)
            sp.dma_start(xs[:, 0:NB - 1, :], x[0:(NB - 1) * P, :].rearrange("(t p) f -> p t f", p=P)).then_inc(s_x_in, 16)
            sp.dma_start(xs[0:TAIL, NB - 1, :], x[(NB - 1) * P:N_NODES, :]).then_inc(s_x_in, 16)
            sp.wait_ge(s_raw_set, 1)
            for k, e in enumerate((src, dst)):
                sp.dma_start(raw[:, k, 0:BLK - 1, :], e[0:full].rearrange("(b p e) -> p b e", p=P, e=P)).then_inc(s_edges_in, 16)
                sp.dma_start(raw[0:rows, k, BLK - 1, :], e[full:full + rows * P].rearrange("(p e) -> p e", e=P)).then_inc(s_edges_in, 16)
                sp.dma_start(raw[rows:rows + 1, k, BLK - 1, 0:rest], e[full + rows * P:N_EDGES].rearrange("(p e) -> p e", p=1)).then_inc(s_edges_in, 16)
            sp.dma_start(w_rows[:, 0, :], w_self).then_inc(s_w_in, 16)
            sp.dma_start(w_rows[:, 1, :], w_neigh).then_inc(s_w_in, 16)
            for k, w in enumerate((qw, kw, vw)):
                sp.dma_start(w_qkv[:, k * D:(k + 1) * D], w).then_inc(s_w_in, 16)
            sp.wait_ge(s_parts, 1)
            sp.dma_start(h_table.rearrange("(t p) f -> p t f", p=P), parts[:, :, :]).then_inc(s_h_table, 16)
            sp.wait_ge(s_windows, 1)
            for k in range(2):
                sp.dma_start(window[0:1, k, 0:BLK * P // GT], ints[0:BLK, k * P // GT:(k + 1) * P // GT]).then_inc(s_window_row, 16)
            for i in range(STEPS7):
                sp.wait_ge(s_kv, i + 1)
                sp.dma_start(kv_table[i * NT7 * P:(i + 1) * NT7 * P, :].rearrange("(t p) f -> p t f", p=P), kv_stage[:, i % 2, :, :]).then_inc(s_kv_table[i % 2], 16)
            sp.wait_ge(s_out_ready, 1)
            sp.dma_start(out[0:(NB - 1) * P, :].rearrange("(t p) f -> p t f", p=P), work[:, 0:NB - 1, :]).then_inc(s_out, 16)
            sp.dma_start(out[(NB - 1) * P:N_NODES, :], work[0:TAIL, NB - 1, :]).then_inc(s_out, 16)
            sp.wait_ge(s_h_table, 16)
            for j in range(2):
                sp.wait_ge(s_kv_table[j], 16 * len(range(j, STEPS7, 2)))
            sp.wait_ge(s_out, 32)

        @block.gpsimd
        def _(pool):
            nc.gpsimd.iota(iota_part_i[:, :], [[0, 1]], base=0, channel_multiplier=1).then_inc(s_iota, 1)
            nc.gpsimd.iota(iota_i, [[1, TILES0]], base=0, channel_multiplier=0).then_inc(s_iota, 1)
            goal = pool.alloc_register("staged_goal")

            def gather(staged, gathered, lo, hi, table, rows):
                with pool.Fori(lo // RING, hi // RING):
                    for u in range(RING):
                        pool.wait_ge(staged, goal)
                        pool.reg_add(goal, goal, 1)
                        for g in range(GT):
                            nc.gpsimd.indirect_dma_start(
                                rows[:, u, g, :], None, table,
                                bass.IndirectOffsetOnAxis(ap=idx_stage[:, u, g:g + 1], axis=0)).then_inc(gathered[u], 16)

            pool.wait_ge(s_h_table, 16)
            pool.reg_mov(goal, 1)
            gather(s_staged0, s_gathered0, 0, RAW_GROUPS, h_table, msg0)
            r = is_slow(pool, "pool_slow")
            with pool.If_ne(r, 0):
                gather(s_staged0, s_gathered0, RAW_GROUPS, GROUPS0, h_table, msg0)
            for j in range(2):
                pool.wait_ge(s_kv_table[j], 16 * len(range(j, STEPS7, 2)))
            pool.reg_mov(goal, 1)
            gather(s_staged1, s_gathered1, 0, GROUPS1, kv_table, msg)

        @block.scalar
        def _(act):
            copy = nc.scalar.copy

            def layer_norm_part(k):
                act.wait_ge(s_centred, k + 1)
                nc.scalar.activation(h[:, :, :], work[:, :, :], ACT.Square).then_inc(s_squared, 1)
                act.wait_ge(s_var, k + 1)
                nc.scalar.activation(stat2[:, :], stat[:, :], ACT.Sqrt, bias=eps_col[:, :], scale=1.0 / D).then_inc(s_sd, 1)

            def stage_cols(b, m, slot):
                copy(cols_stage[:, slot, :, :], cols[:, bass.ds(m * CC, CC), :]).then_inc(b.cols_staged, 1)

            def code_chunk(b, m, slot):
                act.wait_ge(b.cols_staged, m + 1)
                act.wait_ge(b.hot_rows, m + 1)
                act.wait_ge(b.scattered, m + 1)
                for c in range(CC):
                    for part in range(2):
                        last = nc.scalar.mul(code_row[:, slot % 2, c, part, :], hot_row[:, slot % 2, c, :],
                                             cols_stage[:, slot, c, 2 + part:3 + part])
                last.then_inc(b.code_rows, 1)

            def start_codes(b):
                act.wait_ge(b.cols, 1)
                stage_cols(b, 0, 0)
                stage_cols(b, 1, 1)

            def code_steps(b, m, slot):
                code_chunk(b, m, slot)
                copy(cols_stage[:, (slot + 2) % 4, :, :], cols[:, bass.ds(m * CC + 2 * CC, CC), :]).then_inc(b.cols_staged, 1)

            def stage_lists(idx, local, n, u, staged):
                copy(loc_stage[:, u, :], local[:, bass.ds(n * GT, GT)])
                copy(idx_stage[:, u, :], idx[:, bass.ds(n * GT, GT)]).then_inc(staged, 1)

            def restage0(n, u):
                act.wait_ge(s_summed0, n + 1)
                stage_lists(idx0, local0, n + RING, u, s_staged0)

            act.wait_ge(s_x_in, 32)
            act.wait_ge(s_const, 1)
            layer_norm_part(0)
            r = is_slow(act, "act_slow")
            with act.If_ne(r, 0):
                start_codes(BK0)
                with act.Fori(0, CHUNKS // 4) as i:
                    for c in range(4):
                        code_steps(BK0, i * 4 + c, c)
                act.wait_ge(BK0.lists, 1)
            act.wait_ge(s_lists0, 1)
            for n in range(RING):
                stage_lists(idx0, local0, n, n, s_staged0)
            with act.Fori(0, B // RING) as i:
                for u in range(RING):
                    restage0(i * RING + u, u)
            start_codes(BK1)
            with act.Fori(B // RING, C // RING) as i:
                for u in range(RING):
                    n = i * RING + u
                    for c in range(C_CHUNKS):
                        code_steps(BK1, (n - B) * C_CHUNKS + c, (C_CHUNKS * u + c) % 4)
                    restage0(n, u)
            with act.If_ne(r, 0):
                with act.Fori(C // RING, GROUPS0 // RING) as i:
                    for u in range(RING):
                        restage0(i * RING + u, u)

            act.wait_ge(s_neigh, 1)
            for i in range(STEPS7):
                wait(act, s_node_t, i)
                copy(node_stage[:, 0, :, :], h[:, i * NT7:(i + 1) * NT7, :])
                copy(node_stage[:, 1, :, :], work[:, i * NT7:(i + 1) * NT7, :]).then_inc(s_node_staged, 1)
                act.wait_ge(s_node_t, i + 1)
                wait(act, s_dense, i)
                copy(node_t[:, 0, :, :], psA[0:D, 0:NT7 * P].rearrange("p (t e) -> p t e", t=NT7)).then_inc(s_node_t_in, 1)
            act.wait_ge(s_x1, STEPS7)
            layer_norm_part(1)
            act.wait_ge(s_h, 2)
            for i in range(STEPS7):
                wait(act, s_node_t, STEPS7 + i)
                copy(node_stage[:, 0, :, :], h[:, i * NT7:(i + 1) * NT7, :]).then_inc(s_node_staged, 1)
                act.wait_ge(s_node_t, STEPS7 + i + 1)
                wait(act, s_dense, STEPS7 + i)
                copy(node_t[:, 0, :, :], psA[0:D, 0:NT7 * P].rearrange("p (t e) -> p t e", t=NT7)).then_inc(s_node_t_in, 1)

            act.wait_ge(BK1.lists, 1)
            for n in range(RING):
                stage_lists(idx1, local1, n, n, s_staged1)

            def hot_t_out(n, u):
                act.wait_ge(s_hot_t, n + 1)
                wait(act, s_q_edge, n - 1)
                copy(hot_t[:, u % 2, :, :], bank(psA, u % 2).rearrange("p (g e) -> p g e", g=GT)).then_inc(s_hot_t_in, 1)

            def attend_step(n, u):
                act.wait_ge(s_clipped, n + 1)
                wait(act, s_summed1, n - 1)
                nc.scalar.activation(weighted[:, u % 2, :, D:W1],
                                     score[:, u % 2, :].rearrange("p (g h) -> p g h", g=GT), ACT.Exp).then_inc(s_exp, 1)
                hot_t_out(n + 2, u + 2)
                act.wait_ge(s_weighted, n + 1)
                stage_lists(idx1, local1, n + RING, u, s_staged1)

            hot_t_out(0, 0)
            hot_t_out(1, 1)
            rounds(act, GROUPS1, attend_step)

        @block.vector
        def _(dve):
            V = nc.vector
            chain = [0]

            def link(ins, semaphore=s_dve, count=chain):
                count[0] = count[0] + 1
                ins.then_inc(semaphore, 1)
                dve.wait_ge(semaphore, count[0])

            V.memset(xs[:, NB - 1, :], 0.0).then_inc(s_x_set, 1)
            V.memset(raw[:, :, BLK - 1, :], -1).then_inc(s_raw_set, 1)
            V.memset(ones[:, :], 1.0)
            V.memset(ones_h[:, :], 1.0)
            V.memset(zeros_h[:, :], 0.0)
            V.memset(eps_col[:, :], EPS_LN)
            V.memset(parts[:, :, D:MID], 1.0)
            V.memset(parts[:, :, SPLIT - 1:SPLIT], 0.0)
            V.memset(idx1[:, TILES1:], 0)
            V.memset(local1[:, TILES1:], -1.0)
            V.memset(idx0[:, RAWT:], 0)
            V.memset(local0[:, RAWT:], -1.0)
            V.memset(packed1[:, GROUPS1:], 0)
            V.memset(window[:, :, :], 0)
            dve.wait_ge(s_iota, 2)
            V.tensor_copy(iota_part[:, :], iota_part_i[:, :])
            link(V.tensor_copy(iota_f[:, :], iota_i[:, 0:P]))
            V.tensor_copy(iota_b[:, :], iota_i[:, 0:2 * P])
            V.tensor_copy(iota_h[:, :], iota_i[:, :])
            V.tensor_scalar(before[:, :], iota_f[:, :], iota_part[:, :], None, ALU.is_gt)
            V.tensor_scalar(ident[:, :], iota_f[:, :], iota_part[:, :], None, ALU.is_equal).then_inc(s_const, 1)

            bc = lambda ap, n: ap.unsqueeze(2).to_broadcast([P, NB, n])

            def layer_norm(k, source):
                link(V.tensor_reduce(stat[:, :], source[:, :, :], X, ALU.add))
                link(V.tensor_scalar(stat[:, :], stat[:, :], 1.0 / D, None, ALU.mult))
                V.tensor_tensor(work[:, :, :], source[:, :, :], bc(stat[:, :], D), ALU.subtract).then_inc(s_centred, 1)
                dve.wait_ge(s_squared, k + 1)
                V.tensor_reduce(stat[:, :], h[:, :, :], X, ALU.add).then_inc(s_var, 1)
                dve.wait_ge(s_sd, k + 1)
                link(V.reciprocal(stat[:, :], stat2[:, :]))
                link(V.tensor_tensor(work[:, :, :], work[:, :, :], bc(stat[:, :], D), ALU.mult))
                V.tensor_scalar(h[:, :, :], work[:, :, :], 0.0, None, ALU.max).then_inc(s_h, 1)
                dve.wait_ge(s_h, k + 1)

            def split(source, mid, low):
                link(V.tensor_copy(parts[:, :, 0:D], source[:, :, :]))
                link(V.tensor_tensor(work[:, :, :], source[:, :, :], parts[:, :, 0:D], ALU.subtract))
                link(V.tensor_copy(parts[:, :, mid:mid + D], work[:, :, :]))
                return V.tensor_tensor(parts[:, :, low:low + D], work[:, :, :], parts[:, :, mid:mid + D], ALU.subtract)

            dve.wait_ge(s_x_in, 32)
            layer_norm(0, xs)
            split(h, MID, LOW).then_inc(s_parts, 1)

            dve.wait_ge(s_edges_in, 96)
            V.tensor_copy(raw_f, raw).then_inc(s_raw_f, 1)
            dve.wait_ge(s_raw_f, 1)
            dsts = raw_f[:, 1, :, :]
            tile_ends = base[:, 0:2 * BLK].rearrange("p (k b) -> p k b", k=2)
            filled = scan[:, 0:BLK * P].rearrange("p (b e) -> p b e", b=BLK)
            V.tensor_reduce(tile_ends[:, 0, :], dsts, X, ALU.max)
            link(V.tensor_scalar(filled, dsts, 0.0, float(2 * NPAD), ALU.is_lt, ALU.mult))
            link(V.tensor_tensor(filled, filled, dsts, ALU.add))
            V.tensor_reduce(tile_ends[:, 1, :], filled, X, ALU.min).then_inc(s_tile_ends, 1)
            for k, (e, ps) in enumerate(((edge_src, psB), (edge_dst, psC))):
                dve.wait_ge(s_edge_t, k + 1)
                V.tensor_copy(e[:, :], ps[:, 0:BLK * P]).then_inc(s_edge, 1)
            dve.wait_ge(s_w_t, 1)
            V.tensor_copy(w_in[:, :, :], psD[0:D, HALF:HALF + 2 * D].rearrange("p (w f) -> p w f", w=2)).then_inc(s_w_ready, 1)
            dve.wait_ge(s_tile_ends_t, 1)
            G = P // GT
            g_max, g_min = position[0:BLK, 0:G], position[0:BLK, G:2 * G]
            gi_max, gi_min = ints[0:BLK, G:2 * G], ints[0:BLK, 0:G]
            V.tensor_reduce(g_max, psD[0:BLK, 0:P].rearrange("p (g t) -> p g t", t=GT), X, ALU.max)
            link(V.tensor_reduce(g_min, psD[0:BLK, P:2 * P].rearrange("p (g t) -> p g t", t=GT), X, ALU.min))
            V.tensor_copy(gi_max, g_max)
            link(V.tensor_copy(gi_min, g_min))
            V.tensor_scalar(gi_max, gi_max, 7, None, ALU.arith_shift_right)
            link(V.tensor_scalar(gi_min, gi_min, 7, None, ALU.arith_shift_right))
            link(V.tensor_scalar(gi_min, gi_min, NB - 1.0, None, ALU.min))
            link(V.tensor_tensor(g_max, gi_max, gi_min, ALU.subtract))
            V.tensor_scalar(gi_max, g_max, 0.0, None, ALU.is_gt).then_inc(s_windows, 1)
            link(V.tensor_reduce(g_min[:, 0:1], g_max, X, ALU.max))
            V.tensor_scalar(g_span, g_min[:, 0:1], 1.0, None, ALU.is_gt).then_inc(s_windows, 1)
            dve.wait_ge(s_window_all, 1)
            V.tensor_scalar(slow[:, :], psD[0:1, HALF:HALF + 1], 1.0, None, ALU.mult).then_inc(s_wide, 1)
            dve.wait_ge(s_window_row, 32)
            V.tensor_copy(scan[0:1, 0:BLK * G], window[0:1, 0, 0:BLK * G]).then_inc(s_window_f, 1)
            V.scalar_tensor_tensor(window[0:1, 0, 0:BLK * G], window[0:1, 1, 0:BLK * G], float(NEXT), window[0:1, 0, 0:BLK * G], ALU.mult, ALU.add)
            V.tensor_scalar(idx0[:, 0:RAWT], edge_src[:, 0:RAWT], 0.0, None, ALU.max)
            dve.wait_ge(s_window_all, 2)
            V.scalar_tensor_tensor(
                local0[:, 0:RAWT].rearrange("p (g t) -> p g t", t=GT),
                psD[:, 0:RAW_GROUPS].unsqueeze(2).to_broadcast([P, RAW_GROUPS, GT]), -float(P),
                edge_dst[:, 0:RAWT].rearrange("p (g t) -> p g t", t=GT), ALU.mult, ALU.add).then_inc(s_lists0, 1)

            def codes(b, do):
                keys, others = b.key[:, 0:COLS], b.other[:, 0:COLS]
                w, wi = scan[:, 0:COLS], ints[:, 0:COLS]
                do(V.tensor_copy(wi, keys))
                do(V.tensor_scalar(wi, wi, 7, None, ALU.arith_shift_right))
                do(V.tensor_copy(bucket[:, :], wi))
                do(V.tensor_copy(wi, others))
                do(V.tensor_scalar(wi, wi, 10, None, ALU.arith_shift_right))
                do(V.tensor_copy(position[:, :], wi))
                do(V.scalar_tensor_tensor(w, position[:, :], -1024.0, others, ALU.mult, ALU.add))
                do(V.tensor_scalar(cols[:, 0:COLS, 3], w, 1.0 / 1024.0, None, ALU.mult))
                do(V.scalar_tensor_tensor(w, bucket[:, :], -float(P), keys, ALU.mult, ALU.add))
                do(V.tensor_scalar(w, w, 1.0, 8.0, ALU.add, ALU.mult))
                do(V.tensor_tensor(cols[:, 0:COLS, 2], w, position[:, :], ALU.add))
                do(V.memset(position[:, :], 0.0))

            def count_bucket(b, k, do):
                do(V.tensor_scalar(mask[:, :], bucket[:, :], iota_f[:, bass.ds(k, 1)], None, ALU.is_equal, ALU.add,
                                   accum_out=counts[:, bass.ds(k, 1)]))

            def bucket_starts(b, do):
                V.tensor_copy(units_f[:, :], counts[:, :]).then_inc(b.counts, 1)
                dve.wait_ge(b.totals, 1)
                do(V.tensor_scalar(units_i[:, :], psD[:, NB:2 * NB], float((1 << b.unit_shift) - 1), None, ALU.add))
                do(V.tensor_scalar(units_i[:, :], units_i[:, :], b.unit_shift, None, ALU.arith_shift_right))
                do(V.tensor_copy(units_f[:, :], units_i[:, :]))
                V.tensor_tensor_scan(units_end[:, :], ones[:, 0:NB], units_f[:, :], 0.0, ALU.mult, ALU.add).then_inc(b.units_end, 1)
                dve.wait_ge(b.units_end, 1)
                do(V.tensor_tensor(base[:, :], units_end[:, :], units_f[:, :], ALU.subtract))
                do(V.scalar_tensor_tensor(base[:, :], base[:, :], float(1 << b.unit_shift), psD[:, 0:NB], ALU.mult, ALU.add))
                dve.wait_ge(b.end_t, 1)
                do(V.tensor_copy(end_col[0:NB, :], psD[0:NB, HALF:HALF + 1]))
                V.tensor_scalar(past_end[0:NB, 0:b.units], iota_h[0:NB, 0:b.units], end_col[0:NB, :], None, ALU.is_ge).then_inc(b.past_end, 1)

            def unit_buckets(b, do):
                dve.wait_ge(b.unit_bucket_sum, 1)
                do(V.tensor_scalar(b.unit_bucket[:, 0:b.units], psC[0:1, 0:b.units], NB - 1.0, None, ALU.min))

            def place_bucket(b, k, do):
                w = scan[:, 0:COLS]
                do(V.tensor_scalar(mask[:, :], bucket[:, :], iota_f[:, bass.ds(k, 1)], None, ALU.is_equal))
                do(V.tensor_tensor_scan(w, ones[:, 0:1].to_broadcast([P, COLS]), mask[:, :], base[:, bass.ds(k, 1)], ALU.mult, ALU.add))
                do(V.tensor_tensor(w, w, mask[:, :], ALU.mult))
                do(V.tensor_tensor(position[:, :], position[:, :], w, ALU.add))

            def rows_and_tiles(b, do):
                wi = ints[:, 0:COLS]
                do(V.tensor_scalar(position[:, :], position[:, :], -1.0, None, ALU.add))
                do(V.tensor_copy(wi, position[:, :]))
                do(V.tensor_scalar(wi, wi, 7, None, ALU.arith_shift_right))
                do(V.tensor_copy(cols[:, 0:COLS, 1], wi))
                V.scalar_tensor_tensor(cols[:, 0:COLS, 0], cols[:, 0:COLS, 1], -float(P), position[:, :], ALU.mult, ALU.add)
                V.memset(cols[:, COLS:CPAD, :], 0.0).then_inc(b.cols, 1)

            def hot_chunk(b, m, slot):
                dve.wait_ge(b.cols_staged, m + 1)
                dve.wait_ge(b.scattered, m + 1)
                for c in range(CC):
                    last = V.tensor_scalar(hot_row[:, slot % 2, c, :], iota_h[:, 0:P], cols_stage[:, slot, c, 0:1], None, ALU.is_equal)
                last.then_inc(b.hot_rows, 1)
                for c in range(CC):
                    last = V.tensor_scalar(hot_tile[:, slot % 2, c, 0:b.tiles], iota_h[:, 0:b.tiles], cols_stage[:, slot, c, 1:2], None, ALU.is_equal)
                last.then_inc(b.hot_tiles, 1)

            def decode(b, do):
                code = scan[:, 0:b.tiles].bitcast(i32)
                wi = ints[:, 0:b.tiles]
                dve.wait_ge(b.code, 1)
                dve.wait_ge(b.cols_staged, CHUNKS + 2)
                do(V.tensor_scalar(code, psA[:, 0:b.tiles], 1024.0, None, ALU.mult))
                do(V.tensor_scalar(wi, code, 13, None, ALU.arith_shift_right))
                V.tensor_scalar(b.other_idx[:, 0:b.tiles], code, 8191, None, ALU.bitwise_and)
                V.tensor_scalar(b.local[:, 0:b.tiles], wi, -1.0, None, ALU.add).then_inc(b.lists, 1)

            r = is_slow(dve, "dve_slow")
            dve.wait_ge(s_lists0, 1)
            with dve.If_ne(r, 0):
                chain0 = [0]
                do = lambda ins: link(ins, BK0.step, chain0)
                codes(BK0, do)
                start = chain0[0]
                with dve.Fori(0, NB) as k:
                    chain0[0] = k * 1 + start
                    count_bucket(BK0, k, do)
                chain0[0] = start + NB
                bucket_starts(BK0, do)
                unit_buckets(BK0, do)
                do(V.memset(window[:, 1, :], 0))
                start = chain0[0]
                with dve.Fori(0, NB) as k:
                    chain0[0] = k * 4 + start
                    place_bucket(BK0, k, do)
                chain0[0] = start + 4 * NB
                rows_and_tiles(BK0, do)
                with dve.Fori(0, CHUNKS // 4) as i:
                    for c in range(4):
                        hot_chunk(BK0, i * 4 + c, c)
                decode(BK0, do)
                dve.wait_ge(BK0.lists, 1)

            window_reg = dve.alloc_register("window")
            first_bucket = dve.alloc_register("first_bucket")
            two_buckets = dve.alloc_register("two_buckets")

            def make_hot0(n, u):
                dve.wait_ge(s_staged0, n + 1)
                for g in range(GT):
                    ins = V.tensor_scalar(hot0[:, u % RING, g, :], iota_b[:, :], loc_stage[:, u % RING, g:g + 1], None, ALU.is_equal)
                    if g == 0:
                        ins.then_inc(s_added0, 1)
                ins.then_inc(s_hot0, 1)

            def load_window(n):
                dve.reg_load(window_reg, window[0:1, 0, bass.ds(n, 1)])

            def add0(n, u):
                dve.reg_alu(first_bucket, window_reg, NEXT - 1, ALU.bitwise_and)
                dve.reg_alu(two_buckets, window_reg, NEXT, ALU.bitwise_and)
                w = dve.snap(first_bucket, min_val=0, max_val=NB - 1)
                dve.wait_ge(s_summed0, n + 1)
                dve.wait_ge(s_added0, n + 3)
                sums = flat(acc[:, bass.ds(w, 1), 0:W0])
                V.tensor_tensor(sums, sums, bank(psB, u % 2)[:, 0:W0], ALU.add)
                with dve.If_ne(two_buckets, 0):
                    sums = flat(acc[:, bass.ds(w + 1, 1), 0:W0])
                    V.tensor_tensor(sums, sums, bank(psB, u % 2)[:, P:P + W0], ALU.add)

            def group_steps(lo, hi, beside, links):
                start = chain[0]
                with dve.Fori(lo // RING, hi // RING) as i:
                    if links:
                        chain[0] = i * (RING * links) + (start - lo * links)
                    for u in range(RING):
                        n = i * RING + u
                        add0(n, u)
                        make_hot0(n + 1, u + 1)
                        load_window(n + 1)
                        beside(n, u)
                chain[0] = start + (hi - lo) * links

            half = NB // 2
            V.memset(acc[:, 0:half, :], 0.0).then_inc(s_added0, 1)
            V.memset(acc[:, half:, :], 0.0).then_inc(s_added0, 1)
            make_hot0(0, 0)
            load_window(0)
            codes(BK1, link)
            count_bucket(BK1, 0, link)

            def counts_beside(n, u):
                for c in range(A_COUNTS):
                    count_bucket(BK1, n * A_COUNTS + (1 + c), link)
            group_steps(0, A, counts_beside, A_COUNTS)
            bucket_starts(BK1, link)
            unit_buckets(BK1, link)
            tiles_of = bucket1[:, :].rearrange("o (g t) -> o g t", t=GT)
            packed = packed1[:, 0:GROUPS1]
            link(V.scalar_tensor_tensor(packed, tiles_of[:, :, 3], float(NEXT), tiles_of[:, :, 2], ALU.mult, ALU.add))
            link(V.scalar_tensor_tensor(packed, packed, float(NEXT), tiles_of[:, :, 1], ALU.mult, ALU.add))
            link(V.scalar_tensor_tensor(packed, packed, float(NEXT), tiles_of[:, :, 0], ALU.mult, ALU.add))
            place_bucket(BK1, 0, link)
            group_steps(A, B, lambda n, u: place_bucket(BK1, n - (A - 1), link), 4)
            rows_and_tiles(BK1, link)

            def chunks_beside(n, u):
                for c in range(C_CHUNKS):
                    hot_chunk(BK1, (n - B) * C_CHUNKS + (C_CHUNKS + c), (C_CHUNKS * (u + 1) + c) % 4)
            for c in range(C_CHUNKS):
                hot_chunk(BK1, c, c)
            group_steps(B, C, chunks_beside, 0)
            with dve.If_ne(r, 0):
                group_steps(C, GROUPS0, lambda n, u: None, 0)
            decode(BK1, link)
            dve.wait_ge(BK1.lists, 1)

            deg = acc[:, 0:NB, D:W0].rearrange("p t o -> p (t o)")
            link(V.tensor_scalar(stat[:, :], deg, EPS, None, ALU.add))
            link(V.reciprocal(stat[:, :], stat[:, :]))
            link(V.tensor_scalar(work[:, :, :], acc[:, 0:NB, 0:D], EPS, None, ALU.add))
            V.tensor_tensor(work[:, :, :], work[:, :, :], bc(stat[:, :], D), ALU.mult).then_inc(s_neigh, 1)
            for i in range(STEPS7):
                dve.wait_ge(s_node_t, i + 1)
                wait(dve, s_dense, i)
                V.tensor_copy(node_t[:, 1, :, :], psB[0:D, 0:NT7 * P].rearrange("p (t e) -> p t e", t=NT7)).then_inc(s_node_t_in, 1)
                dve.wait_ge(s_dense, i + 1)
                for k, (a, b) in enumerate(((0, PER), (PER, NT7))):
                    xt = xs[:, i * NT7 + a:i * NT7 + b, :]
                    last = V.tensor_tensor(xt, xt, bank(psC, k)[:, 0:(b - a) * D].rearrange("p (t f) -> p t f", f=D), ALU.add)
                last.then_inc(s_x1, 1)
            dve.wait_ge(s_x1, STEPS7)
            layer_norm(1, xs)
            for i in range(STEPS7):
                dve.wait_ge(s_dense, STEPS7 + i + 1)
                if i >= 2:
                    dve.wait_ge(s_kv_table[i % 2], 16 * (i // 2))
                for k, (a, b) in enumerate(((0, PER), (PER, NT7))):
                    V.tensor_copy(work[:, i * NT7 + a:i * NT7 + b, :], bank(psB, k)[:, 0:(b - a) * D].rearrange("p (t f) -> p t f", f=D))
                for k in range(4):
                    a, b = 2 * k, min(2 * k + 2, NT7)
                    last = V.tensor_copy(kv_stage[:, i % 2, a:b, :], bank(psC if k < 2 else psD, k % 2)[:, 0:(b - a) * 2 * D].rearrange("p (t f) -> p t f", f=2 * D))
                last.then_inc(s_kv, 1)
            dve.wait_ge(s_kv, STEPS7)
            split(work, D, 2 * D).then_inc(s_q, 1)

            link(V.memset(acc[:, :, :], 0.0))
            tile_regs = [dve.alloc_register(f"tile_bucket{g}") for g in range(GT)]

            def hot1_tile(n, u, g):
                if g == 0:
                    dve.wait_ge(s_staged1, n + 1)
                ins = V.tensor_scalar(hot[:, u % RING, g, :], iota_f[:, :], loc_stage[:, u % RING, g:g + 1], None, ALU.is_equal)
                if g == GT - 1:
                    ins.then_inc(s_hot1, 1)

            def add1_tile(n, u, g):
                b = dve.snap(tile_regs[g], min_val=0, max_val=NB - 1)
                sums = flat(acc[:, bass.ds(b, 1), :])
                if g == 0:
                    dve.wait_ge(s_summed1, n + 1)
                wait(dve, s_added1, n * GT + g)
                V.tensor_tensor(sums, sums, bank(psC, u % 2)[:, g * W1:(g + 1) * W1], ALU.add).then_inc(s_added1, 1)

            packed_reg = dve.alloc_register("packed")

            def load_buckets(n):
                dve.reg_load(packed_reg, packed1[0:1, bass.ds(n, 1)])
                unpack(dve, tile_regs, packed_reg)

            LINKS1 = 2

            def attend_step(n, u):
                first = isinstance(n, int) and n == 0
                dve.wait_ge(s_q_edge, n + 1)
                dve.wait_ge(s_gathered1[u], arrived(n, u))
                link(V.tensor_tensor(prod[:, :, :], bank(psB, u % 2)[:, 0:GT * D].rearrange("p (g f) -> p g f", g=GT),
                                     msg[:, u, :, 0:D], ALU.mult))
                link(V.tensor_reduce(score[:, u % 2, :], prod[:, :, :].rearrange("p g (h d) -> p (g h) d", d=DH), X, ALU.add))
                V.tensor_scalar(score[:, u % 2, :], score[:, u % 2, :], -10.0, 10.0, ALU.max, ALU.min).then_inc(s_clipped, 1)
                for g in range(GT):
                    if not first:
                        add1_tile(n - 1, u - 1, g)
                    hot1_tile(n + 2, u + 2, g)
                dve.wait_ge(s_exp, n + 1)
                wait(dve, s_summed1, n - 1)
                V.tensor_tensor(weighted[:, u % 2, :, 0:D].rearrange("p g (h d) -> p g h d", h=HEADS),
                                msg[:, u, :, D:2 * D].rearrange("p g (h d) -> p g h d", h=HEADS),
                                weighted[:, u % 2, :, D:W1].unsqueeze(3).to_broadcast([P, GT, HEADS, DH]),
                                ALU.mult).then_inc(s_weighted, 1)
                load_buckets(n)

            def arrived(n, u):
                return (n - u) * (16 * GT // RING) + 16 * GT

            dve.wait_ge(s_q, 1)
            for g in range(GT):
                hot1_tile(0, 0, g)
            for g in range(GT):
                hot1_tile(1, 1, g)
            start = chain[0]
            for n in range(RING):
                attend_step(n, n)
            with dve.Fori(1, GROUPS1 // RING) as i:
                chain[0] = i * (LINKS1 * RING) + start
                for u in range(RING):
                    attend_step(i * RING + u, u)
            chain[0] = start + LINKS1 * GROUPS1
            for g in range(GT):
                add1_tile(GROUPS1 - 1, RING - 1, g)
            dve.wait_ge(s_added1, TILES1)
            link(V.tensor_scalar(rec[:, :, :], acc[:, 0:NB, D:W1], EPS, None, ALU.add))
            link(V.reciprocal(rec[:, :, :], rec[:, :, :]))
            V.tensor_tensor(xs[:, :, :], xs[:, :, :], h[:, :, :], ALU.add)
            link(V.tensor_tensor(work[:, :, :].rearrange("p t (h d) -> p t h d", h=HEADS),
                                 acc[:, 0:NB, 0:D].rearrange("p t (h d) -> p t h d", h=HEADS),
                                 rec[:, :, :].unsqueeze(3).to_broadcast([P, NB, HEADS, DH]), ALU.mult))
            V.tensor_tensor(work[:, :, :], work[:, :, :], xs[:, :, :], ALU.add).then_inc(s_out_ready, 1)

        @block.tensor
        def _(pe):
            mm = nc.tensor.matmul
            T = nc.tensor.transpose
            pe.wait_ge(s_const, 1)
            pe.wait_ge(s_w_in, 80)
            for k in range(2):
                last = T(psD[0:D, HALF + k * D:HALF + (k + 1) * D], w_rows[:, k, :], ident[0:D, 0:D])
            last.then_inc(s_w_t, 1)
            pe.wait_ge(s_raw_f, 1)
            for k, ps in ((0, psB), (1, psC)):
                for b in range(BLK):
                    last = T(ps[:, b * P:(b + 1) * P], raw_f[:, k, b, :], ident[:, :])
                last.then_inc(s_edge_t, 1)
            pe.wait_ge(s_tile_ends, 1)
            for k in range(2):
                last = T(psD[0:BLK, k * P:(k + 1) * P], base[:, k * BLK:(k + 1) * BLK], ident[:, :])
            last.then_inc(s_tile_ends_t, 1)
            pe.wait_ge(s_w_ready, 1)
            pe.wait_ge(s_windows, 2)
            mm(psD[0:1, HALF:HALF + 1], ones[0:BLK, 0:1], g_span, start=True, stop=True).then_inc(s_window_all, 1)
            pe.wait_ge(s_window_f, 1)
            mm(psD[:, 0:BLK * P // GT], ones[0:1, :], scan[0:1, 0:BLK * P // GT], start=True, stop=True).then_inc(s_window_all, 1)

            def bucket_totals(b):
                pe.wait_ge(b.counts, 1)
                mm(psD[:, 0:NB], before[:, :], counts[:, :], start=True, stop=True)
                mm(psD[:, NB:2 * NB], ones[:, :], counts[:, :], start=True, stop=True).then_inc(b.totals, 1)
                pe.wait_ge(b.units_end, 1)
                mm(psD[0:NB, HALF:HALF + 1], units_end[0:1, :], ones[0:1, 0:1], start=True, stop=True).then_inc(b.end_t, 1)
                pe.wait_ge(b.past_end, 1)
                for lo, hi in halves(b.units):
                    last = mm(psC[0:1, lo:hi], ones_h[0:NB, :], past_end[0:NB, lo:hi], start=True, stop=True)
                last.then_inc(b.unit_bucket_sum, 1)

            def start_scatter(b):
                for lo, hi in halves(b.tiles):
                    mm(psA[:, lo:hi], zeros_h[:, :], iota_h[:, lo:hi], start=True, stop=False).then_inc(b.scattered, 1)

            def scatter_chunk(b, m, slot):
                pe.wait_ge(b.hot_tiles, m + 1)
                pe.wait_ge(b.code_rows, m + 1)
                for c in range(CC):
                    for part in range(2):
                        for lo, hi in halves(b.tiles):
                            last = mm(psA[:, lo:hi], code_row[:, slot % 2, c, part, :], hot_tile[:, slot % 2, c, lo:hi],
                                      start=False, stop=False)
                last.then_inc(b.scattered, 1)

            def end_scatter(b):
                for lo, hi in halves(b.tiles):
                    last = mm(psA[:, lo:hi], zeros_h[:, :], iota_h[:, lo:hi], start=False, stop=True)
                last.then_inc(b.code, 1)

            r = is_slow(pe, "pe_slow")
            with pe.If_ne(r, 0):
                bucket_totals(BK0)
                start_scatter(BK0)
                with pe.Fori(0, CHUNKS // 4) as i:
                    for c in range(4):
                        scatter_chunk(BK0, i * 4 + c, c)
                end_scatter(BK0)
                pe.wait_ge(BK0.lists, 1)
            pe.wait_ge(s_lists0, 1)

            two_buckets = pe.alloc_register("pe_two_buckets")

            def sum0_half(n, u, half):
                o = bank(psB, u % 2)[:, half * P:half * P + W0]
                for g in range(GT):
                    for k, (lo, hi) in enumerate(((0, W0), (MID, MID + D), (LOW, LOW + D))):
                        last = mm(o[:, 0:hi - lo], hot0[:, u, g, half * P:(half + 1) * P], msg0[:, u, g, lo:hi],
                                  start=(g == 0 and k == 0), stop=(g == GT - 1 and k == 2))
                return last

            def sum_group0(n, u):
                pe.reg_load(two_buckets, window[0:1, 1, bass.ds(n, 1)])
                pe.wait_ge(s_hot0, n + 1)
                pe.wait_ge(s_gathered0[u], (n - u) * (16 * GT // RING) + 16 * GT)
                pe.wait_ge(s_added0, n + 2)
                with pe.If_ne(two_buckets, 0):
                    sum0_half(n, u, 1)
                sum0_half(n, u, 0).then_inc(s_summed0, 1)

            with pe.Fori(0, A // RING) as i:
                for u in range(RING):
                    sum_group0(i * RING + u, u)
            bucket_totals(BK1)
            with pe.Fori(A // RING, B // RING) as i:
                for u in range(RING):
                    sum_group0(i * RING + u, u)
            start_scatter(BK1)
            with pe.Fori(B // RING, C // RING) as i:
                for u in range(RING):
                    n = i * RING + u
                    sum_group0(n, u)
                    for c in range(C_CHUNKS):
                        scatter_chunk(BK1, (n - B) * C_CHUNKS + c, (C_CHUNKS * u + c) % 4)
            end_scatter(BK1)
            with pe.If_ne(r, 0):
                with pe.Fori(C // RING, GROUPS0 // RING) as i:
                    for u in range(RING):
                        sum_group0(i * RING + u, u)

            pe.wait_ge(BK1.lists, 1)
            for i in range(STEPS7):
                pe.wait_ge(s_node_staged, i + 1)
                wait(pe, s_node_t_in, 2 * i)
                for k, ps in ((0, psA), (1, psB)):
                    for t in range(NT7):
                        last = T(ps[0:D, t * P:(t + 1) * P], node_stage[:, k, t, :], ident[:, :])
                last.then_inc(s_node_t, 1)
                pe.wait_ge(s_node_t_in, 2 * (i + 1))
                wait(pe, s_x1, i)
                for t in range(NT7):
                    o = bank(psC, t // PER)[:, (t % PER) * D:(t % PER + 1) * D]
                    mm(o, node_t[:, 0, t, :], w_in[:, 0, :], start=True, stop=False)
                    last = mm(o, node_t[:, 1, t, :], w_in[:, 1, :], start=False, stop=True)
                last.then_inc(s_dense, 1)
            for i in range(STEPS7):
                pe.wait_ge(s_node_staged, STEPS7 + i + 1)
                for t in range(NT7):
                    last = T(psA[0:D, t * P:(t + 1) * P], node_stage[:, 0, t, :], ident[:, :])
                last.then_inc(s_node_t, 1)
                pe.wait_ge(s_node_t_in, 2 * STEPS7 + i + 1)
                wait(pe, s_kv, i)
                for t in range(NT7):
                    mm(bank(psB, t // PER)[:, (t % PER) * D:(t % PER + 1) * D], node_t[:, 0, t, :], w_qkv[:, 0:D], start=True, stop=True)
                    last = mm(bank(psC if t < 4 else psD, t // 2 % 2)[:, (t % 2) * 2 * D:(t % 2 + 1) * 2 * D], node_t[:, 0, t, :],
                              w_qkv[:, D:3 * D], start=True, stop=True)
                last.then_inc(s_dense, 1)

            q_packed = pe.alloc_register("q_packed")
            q_regs = [pe.alloc_register(f"q_bucket{g}") for g in range(GT)]

            def load_q_buckets(n):
                pe.reg_load(q_packed, packed1[0:1, bass.ds(n, 1)])
                unpack(pe, q_regs, q_packed)

            def transpose_hot(n, u):
                pe.wait_ge(s_hot1, n + 1)
                wait(pe, s_hot_t_in, n - 1)
                for g in range(GT):
                    last = T(bank(psA, u % 2)[:, g * P:(g + 1) * P], hot[:, u % RING, g, :], ident[:, :])
                last.then_inc(s_hot_t, 1)

            def q_of_edges(n, u):
                pe.wait_ge(s_hot_t_in, n + 1)
                wait(pe, s_clipped, n - 1)
                for g in range(GT):
                    b = pe.snap(q_regs[g], min_val=0, max_val=NB - 1)
                    for k in range(3):
                        last = mm(bank(psB, u % 2)[:, g * D:(g + 1) * D], hot_t[:, u % 2, g, :],
                                  flat(parts[:, bass.ds(b, 1), k * D:(k + 1) * D]), start=(k == 0), stop=(k == 2))
                last.then_inc(s_q_edge, 1)

            def sum_weighted(n, u):
                pe.wait_ge(s_weighted, n + 1)
                wait(pe, s_added1, (n - 1) * GT)
                for g in range(GT):
                    last = mm(bank(psC, u % 2)[:, g * W1:(g + 1) * W1], hot[:, u, g, :], weighted[:, u % 2, g, :], start=True, stop=True)
                last.then_inc(s_summed1, 1)

            transpose_hot(0, 0)
            transpose_hot(1, 1)
            pe.wait_ge(s_q, 1)
            load_q_buckets(0)
            q_of_edges(0, 0)
            load_q_buckets(1)

            def attend_step(n, u):
                q_of_edges(n + 1, u + 1)
                load_q_buckets(n + 2)
                transpose_hot(n + 2, u + 2)
                sum_weighted(n, u)
            rounds(pe, GROUPS1, attend_step)


def kernel(x, src, dst, L0_gnn_W_self, L0_gnn_W_neigh, L1_gnn_qW, L1_gnn_kW, L1_gnn_vW):
    import numpy as np
    import concourse.bacc as bacc
    from concourse.bass_utils import run_bass_kernel_spmd

    nc = bacc.Bacc("TRN2", target_bir_lowering=False, num_devices=1)
    given = dict(x=x, src=src, dst=dst, w_self=L0_gnn_W_self, w_neigh=L0_gnn_W_neigh, qw=L1_gnn_qW, kw=L1_gnn_kW, vw=L1_gnn_vW)
    arrays, args = {}, []
    for name, a in given.items():
        a = np.ascontiguousarray(a)
        arrays["in_" + name] = a
        args.append(nc.dram_tensor("in_" + name, a.shape, mybir.dt.from_np(a.dtype), kind="ExternalInput").ap())
    h_table = nc.dram_tensor("h_table", (NPAD, SPLIT), mybir.dt.bfloat16, kind="Internal").ap()
    kv_table = nc.dram_tensor("kv_table", (NPAD, 2 * D), mybir.dt.float32, kind="Internal").ap()
    out = nc.dram_tensor("out", (N_NODES, D), mybir.dt.float32, kind="ExternalOutput").ap()
    gnn_program(nc, *args, h_table, kv_table, out)
    r = run_bass_kernel_spmd(nc, [arrays], core_ids=[0])
    return r.results[0]["out"]
```

```python
import concourse.bass as bass
from concourse import mybir
from contextlib import ExitStack

P = 128
N_NODES = 6250
N_EDGES = 100000
D = 96
HEADS = 4
DH = D // HEADS
EPS_LN = 1e-5
EPS = 1e-8
NB = -(-N_NODES // P)
NPAD = NB * P
TAIL = N_NODES - (NB - 1) * P
BLK = -(-(-(-N_EDGES // P)) // P)
GT = 4
RAWT = -(-(-(-N_EDGES // P)) // GT) * GT
RAW_GROUPS = RAWT // GT
RING = 4
GROUPS0 = -(-((N_EDGES + NB * (GT * P - 1)) // (GT * P)) // RING) * RING
TILES0 = GROUPS0 * GT
TILES1 = -(-((N_EDGES + NB * (P - 1)) // P) // (GT * RING)) * GT * RING
GROUPS1 = TILES1 // GT
AHEAD = RING * GT
NEXT = 64
A_COUNTS = 4
A_GROUPS = (NB - 1) // A_COUNTS
B_PLACED = 2
B_GROUPS = (NB - 1) // B_PLACED
C_GROUPS = RAW_GROUPS - A_GROUPS - B_GROUPS
CHUNKS = C_GROUPS
CC = -(-RAWT // CHUNKS)
COLS = CHUNKS * CC
assert CHUNKS % 4 == 0 and A_GROUPS * A_COUNTS == B_GROUPS * B_PLACED == NB - 1 and NB % 4 == 1 and A_COUNTS < CC
assert A_GROUPS % RING == B_GROUPS % RING == C_GROUPS % RING == 0 and COLS <= BLK * P
W0 = D + 1
SPLIT = 3 * D + 2
MID, LOW = D + 1, 2 * D + 1
W1 = D + HEADS
NT7 = 7
STEPS7 = NB // NT7
LOADS = ((0, 2), (2, 5), (5, STEPS7))
HALF = 512
assert NB <= NEXT and GT * 6 <= 24 and NB % NT7 == 0 and max(TILES0, TILES1) <= 2 * HALF


class Bucketing:

    def __init__(self, name, sem, key, other, unit_shift, units, lists, unit_bucket):
        self.key, self.other = key, other
        self.unit_shift, self.units, self.tiles = unit_shift, units, (units << unit_shift) // P
        self.other_idx, self.local = lists
        self.unit_bucket = unit_bucket
        self.step = sem(f"s_{name}_step")
        self.counts = sem(f"s_{name}_counts")
        self.totals = sem(f"s_{name}_totals")
        self.units_end = sem(f"s_{name}_units_end")
        self.end_t = sem(f"s_{name}_end_t")
        self.past_end = sem(f"s_{name}_past_end")
        self.place = sem(f"s_{name}_place")
        self.unit_bucket_sum = sem(f"s_{name}_unit_bucket_sum")
        self.cols = sem(f"s_{name}_cols")
        self.cols_staged = sem(f"s_{name}_cols_staged")
        self.hot_rows = sem(f"s_{name}_hot_rows")
        self.hot_tiles = sem(f"s_{name}_hot_tiles")
        self.code_rows = sem(f"s_{name}_code_rows")
        self.scattered = sem(f"s_{name}_scattered")
        self.code = sem(f"s_{name}_code")
        self.lists = sem(f"s_{name}_lists")


def gnn_program(nc, x, src, dst, w_self, w_neigh, qw, kw, vw, h_table, kv_table, out):
    f32, i32, u16, f16, bf16 = mybir.dt.float32, mybir.dt.int32, mybir.dt.uint16, mybir.dt.float16, mybir.dt.bfloat16
    ALU = mybir.AluOpType
    ACT = mybir.ActivationFunctionType
    X = mybir.AxisListType.X

    with ExitStack() as ctx:
        def sb(name, shape, dt):
            return ctx.enter_context(nc.sbuf_tensor(name, shape, dt))

        def sem(name):
            return ctx.enter_context(nc.semaphore(name))

        iota_h = sb("iota_h", [P, TILES0], f16)
        iota_f = sb("iota_f", [P, P], f32)
        iota_b = sb("iota_b", [P, 2 * P], bf16)
        iota_part_i = sb("iota_part_i", [P, 1], i32)
        iota_part = sb("iota_part", [P, 1], f32)
        ident = sb("ident", [P, P], f32)
        before = sb("before", [P, P], f32)
        ones = sb("ones", [P, P], f32)
        ones_h = sb("ones_h", [P, 1], f16)
        zeros_h = sb("zeros_h", [P, P], f16)
        eps_col = sb("eps_col", [P, 1], f32)
        w_rows = sb("w_rows", [D, 2, D], f32)
        w_in = sb("w_in", [D, 2, D], f32)
        w_qkv = sb("w_qkv", [D, 3 * D], f32)
        edge_src = sb("edge_src", [P, BLK * P], f32)
        edge_dst = sb("edge_dst", [P, BLK * P], f32)
        mask = sb("mask", [P, 4, COLS], f16)
        scan = sb("scan", [P, TILES0], f32)
        position = sb("position", [P, COLS], f32)
        counts = sb("counts", [P, NB], f32)
        units_i = sb("units_i", [P, NB], i32)
        units_f = sb("units_f", [P, NB], f32)
        units_end = sb("units_end", [P, NB], f32)
        base = sb("base", [P, NB], f32)
        end_col = sb("end_col", [P, 1], f32)
        cols_stage = sb("cols_stage", [P, 4, CC, 4], f32)
        idx0 = sb("idx0", [P, TILES0 + AHEAD], i32)
        local0 = sb("local0", [P, TILES0 + AHEAD], f32)
        idx1 = sb("idx1", [P, TILES1 + AHEAD], i32)
        local1 = sb("local1", [P, TILES1 + AHEAD], f32)
        window = sb("window", [1, 2, 2 * P], i32)
        bucket1 = sb("bucket1", [1, TILES1], i32)
        packed1 = sb("packed1", [1, GROUPS1 + RING], i32)
        slow = sb("slow", [1, 1], i32)
        xs = sb("xs", [P, NB, D], f32)
        h = sb("h", [P, NB, D], f32)
        work = sb("work", [P, NB, D], f32)
        parts = sb("parts", [P, NB, SPLIT], bf16)
        stat = sb("stat", [P, NB], f32)
        stat2 = sb("stat2", [P, NB], f32)
        acc = sb("acc", [P, NB + 1, W1], f32)
        rec = sb("rec", [P, NB, HEADS], f32)
        idx_stage = sb("idx_stage", [P, RING, GT], i32)
        loc_stage = sb("loc_stage", [P, RING, GT], f32)
        msg = sb("msg", [P, RING, GT, 2 * D], f32)
        hot = sb("hot", [P, RING, GT, P], f32)
        hot_t = sb("hot_t", [P, 2, GT, P], bf16)
        prod = sb("prod", [P, GT, D], f32)
        score = sb("score", [P, 2, GT * HEADS], f32)
        weighted = sb("weighted", [P, 2, GT, W1], f32)
        node_t = sb("node_t", [D, 2, NT7, P], f32)

        flat = lambda t: t.rearrange("p a f -> p (a f)")
        flat3 = lambda t: t.rearrange("p a b f -> p (a b f)")
        raw = flat3(hot[:, :, :, :])[:, 0:2 * BLK * P].bitcast(i32).rearrange("p (k b e) -> p k b e", k=2, b=BLK)
        raw_f = flat3(msg[:, :, :, :])[:, 0:2 * BLK * P].rearrange("p (k b e) -> p k b e", k=2, b=BLK)
        iota_i = flat3(msg[:, :, :, :])[:, 2 * BLK * P:2 * BLK * P + TILES0].bitcast(i32)
        msg0 = flat3(msg[:, :, :, :])[:, 0:RING * GT * SPLIT // 2].bitcast(bf16).rearrange("p (r g f) -> p r g f", r=RING, g=GT)
        hot0 = flat3(hot[:, :, :, :]).bitcast(bf16).rearrange("p (r g e) -> p r g e", r=RING, g=GT)
        kv_stage = flat3(msg[:, :, :, :])[:, 0:4 * NT7 * D].rearrange("p (k t f) -> p k t f", k=2, t=NT7)
        CPAD = COLS + 3 * CC
        cols = flat(work[:, :, :])[:, 0:4 * CPAD].rearrange("p (t c) -> p t c", c=4)
        ints = flat(work[:, :, :])[:, 4 * CPAD:4 * CPAD + TILES0].bitcast(i32)
        bucket = flat(work[:, :, :])[:, 4 * CPAD + TILES0:4 * CPAD + TILES0 + COLS // 2].bitcast(f16)
        parts_h = flat(parts[:, :, :]).bitcast(f16)
        TILE_END, CODE_END, ROW_END = 2 * CC * TILES0, 2 * CC * (TILES0 + 2 * P), 2 * CC * (TILES0 + 3 * P)
        assert ROW_END <= NB * SPLIT
        hot_tile = parts_h[:, 0:TILE_END].rearrange("p (s c t) -> p s c t", s=2, c=CC)
        code_row = parts_h[:, TILE_END:CODE_END].rearrange("p (s c k e) -> p s c k e", s=2, c=CC, k=2)
        hot_row = parts_h[:, CODE_END:ROW_END].rearrange("p (s c e) -> p s c e", s=2, c=CC)
        past_end = hot_tile[:, 0, 0, :]
        g_span = units_f[0:BLK, 0:1]
        g_window = mask[0:BLK, 0, 0:4 * P // GT].bitcast(i32)

        psA = ctx.enter_context(nc.psum_tensor("psA", [P, 2 * HALF], f32))
        psB = ctx.enter_context(nc.psum_tensor("psB", [P, 2 * HALF], f32))
        psC = ctx.enter_context(nc.psum_tensor("psC", [P, 2 * HALF], f32))
        psD = ctx.enter_context(nc.psum_tensor("psD", [P, 2 * HALF], f32))

        BK0 = Bucketing("bk0", sem, edge_dst, edge_src, 9, GROUPS0, (idx0, local0), window[:, 0, :])
        BK1 = Bucketing("bk1", sem, edge_src, edge_dst, 7, TILES1, (idx1, local1), bucket1[:, :])

        s_raw_set = sem("s_raw_set")
        s_edges_in = sem("s_edges_in")
        s_x_set = sem("s_x_set")
        s_x_in = [sem(f"s_x_in{i}") for i in range(len(LOADS))]
        s_w_in = sem("s_w_in")
        s_iota = sem("s_iota")
        s_const = sem("s_const")
        s_dve = sem("s_dve")
        s_raw_f = sem("s_raw_f")
        s_edge_t = sem("s_edge_t")
        s_edge = sem("s_edge")
        s_w_t = sem("s_w_t")
        s_w_ready = sem("s_w_ready")
        s_row_sum = sem("s_row_sum")
        s_centred = sem("s_centred")
        s_squared = sem("s_squared")
        s_var = sem("s_var")
        s_sd = sem("s_sd")
        s_rstd = sem("s_rstd")
        s_h = sem("s_h")
        s_high = sem("s_high")
        s_rest = sem("s_rest")
        s_mid = sem("s_mid")
        s_parts = sem("s_parts")
        s_h_table = sem("s_h_table")
        s_tile_ends = sem("s_tile_ends")
        s_tile_ends_t = sem("s_tile_ends_t")
        s_windows = sem("s_windows")
        s_window_row = sem("s_window_row")
        s_window_f = sem("s_window_f")
        s_window_all = sem("s_window_all")
        s_wide = sem("s_wide")
        s_lists0 = sem("s_lists0")
        s_staged0 = sem("s_staged0")
        s_gathered0 = [sem(f"s_gathered0_{i}") for i in range(RING)]
        s_gathered1 = [sem(f"s_gathered1_{i}") for i in range(RING)]
        s_hot0 = sem("s_hot0")
        s_summed0 = sem("s_summed0")
        s_added0 = sem("s_added0")
        s_mean = sem("s_mean")
        s_node_t = sem("s_node_t")
        s_node_t_in = sem("s_node_t_in")
        s_dense = sem("s_dense")
        s_x_self = sem("s_x_self")
        s_x1 = sem("s_x1")
        s_q_made = sem("s_q_made")
        s_kv_made_low = sem("s_kv_made_low")
        s_kv_made = sem("s_kv_made")
        s_kv_low = sem("s_kv_low")
        s_kv_high = sem("s_kv_high")
        s_residual = sem("s_residual")
        s_kv_table = [sem(f"s_kv_table{i}") for i in range(2)]
        s_staged1 = sem("s_staged1")
        s_hot1 = sem("s_hot1")
        s_hot_t = sem("s_hot_t")
        s_hot_t_in = sem("s_hot_t_in")
        s_q_edge = sem("s_q_edge")
        s_clipped = sem("s_clipped")
        s_exp = sem("s_exp")
        s_weighted = sem("s_weighted")
        s_summed1 = sem("s_summed1")
        s_added1 = sem("s_added1")
        s_out_ready = sem("s_out_ready")
        s_out = sem("s_out")

        block = ctx.enter_context(nc.Block())

        def wait(eng, semaphore, value):
            if not isinstance(value, int) or value > 0:
                eng.wait_ge(semaphore, value)

        def rounds(eng, count, step):
            for n in range(RING):
                step(n, n)
            with eng.Fori(1, count // RING) as i:
                for u in range(RING):
                    step(i * RING + u, u)

        def is_slow(eng, name):
            eng.wait_ge(s_wide, 1)
            r = eng.alloc_register(name)
            eng.reg_load(r, slow[0:1, 0:1])
            return r

        def unpack(eng, regs, packed):
            for g, reg in enumerate(regs):
                if g:
                    eng.reg_alu(reg, packed, 6 * g, ALU.logical_shift_right)
                eng.reg_alu(reg, reg if g else packed, NEXT - 1, ALU.bitwise_and)

        bank = lambda ps, k: ps[:, k * HALF:(k + 1) * HALF]
        halves = lambda n: ((0, HALF), (HALF, n)) if n > HALF else ((0, n),)
        tiles_of_step = lambda i: slice(i * NT7, (i + 1) * NT7)
        PER = HALF // D
        A, B, C = A_GROUPS, A_GROUPS + B_GROUPS, RAW_GROUPS

        @block.sync
        def _(sp):
            by_tile = lambda t: t.rearrange("(t p) f -> p t f", p=P)

            def rows_of(a, b, each):
                whole = min(b * NT7, NB - 1)
                each(slice(a * NT7 * P, whole * P), slice(a * NT7, whole))
                if b == STEPS7:
                    each(slice(whole * P, N_NODES), None)

            full = (BLK - 1) * P * P
            rows = (N_EDGES - full) // P
            rest = N_EDGES - full - rows * P
            sp.wait_ge(s_raw_set, 1)
            for k, e in enumerate((src, dst)):
                sp.dma_start(raw[:, k, 0:BLK - 1, :], e[0:full].rearrange("(b p e) -> p b e", p=P, e=P)).then_inc(s_edges_in, 16)
                sp.dma_start(raw[0:rows, k, BLK - 1, :], e[full:full + rows * P].rearrange("(p e) -> p e", e=P)).then_inc(s_edges_in, 16)
                sp.dma_start(raw[rows:rows + 1, k, BLK - 1, 0:rest], e[full + rows * P:N_EDGES].rearrange("(p e) -> p e", p=1)).then_inc(s_edges_in, 16)
            sp.wait_ge(s_x_set, 1)
            for c, (a, b) in enumerate(LOADS):
                def load(rows, tiles):
                    if tiles:
                        sp.dma_start(xs[:, tiles, :], by_tile(x[rows, :])).then_inc(s_x_in[c], 16)
                    else:
                        sp.dma_start(xs[0:TAIL, NB - 1, :], x[rows, :]).then_inc(s_x_in[c], 16)
                rows_of(a, b, load)
            sp.dma_start(w_rows[:, 0, :], w_self).then_inc(s_w_in, 16)
            sp.dma_start(w_rows[:, 1, :], w_neigh).then_inc(s_w_in, 16)
            for k, w in enumerate((qw, kw, vw)):
                sp.dma_start(w_qkv[:, k * D:(k + 1) * D], w).then_inc(s_w_in, 16)
            sp.wait_ge(s_windows, 1)
            for k in range(2):
                sp.dma_start(window[0:1, k, 0:BLK * P // GT], g_window[:, k * P // GT:(k + 1) * P // GT]).then_inc(s_window_row, 16)
            for i in range(STEPS7):
                sp.wait_ge(s_parts, i + 1)
                sp.dma_start(by_tile(h_table[i * NT7 * P:(i + 1) * NT7 * P, :]), parts[:, tiles_of_step(i), :]).then_inc(s_h_table, 16)
            for i in range(STEPS7):
                sp.wait_ge(s_kv_low, i + 1)
                sp.wait_ge(s_kv_high, i + 1)
                sp.dma_start(by_tile(kv_table[i * NT7 * P:(i + 1) * NT7 * P, :]), kv_stage[:, i % 2, :, :]).then_inc(s_kv_table[i % 2], 16)
            for i in range(STEPS7):
                sp.wait_ge(s_out_ready, i + 1)

                def store(rows, tiles):
                    if tiles:
                        sp.dma_start(by_tile(out[rows, :]), work[:, tiles, :]).then_inc(s_out, 16)
                    else:
                        sp.dma_start(out[rows, :], work[0:TAIL, NB - 1, :]).then_inc(s_out, 16)
                rows_of(i, i + 1, store)
            sp.wait_ge(s_h_table, 16 * STEPS7)
            for j in range(2):
                sp.wait_ge(s_kv_table[j], 16 * len(range(j, STEPS7, 2)))
            sp.wait_ge(s_out, 16 * (STEPS7 + 1))

        @block.gpsimd
        def _(pool):
            nc.gpsimd.iota(iota_part_i[:, :], [[0, 1]], base=0, channel_multiplier=1).then_inc(s_iota, 1)
            nc.gpsimd.iota(iota_i, [[1, TILES0]], base=0, channel_multiplier=0).then_inc(s_iota, 1)
            goal = pool.alloc_register("staged_goal")

            def gather(staged, gathered, lo, hi, table, rows):
                with pool.Fori(lo // RING, hi // RING):
                    for u in range(RING):
                        pool.wait_ge(staged, goal)
                        pool.reg_add(goal, goal, 1)
                        for g in range(GT):
                            nc.gpsimd.indirect_dma_start(
                                rows[:, u, g, :], None, table,
                                bass.IndirectOffsetOnAxis(ap=idx_stage[:, u, g:g + 1], axis=0)).then_inc(gathered[u], 16)

            def low_part(k, i, low):
                t = tiles_of_step(i)
                pool.wait_ge(s_mid, k * STEPS7 + i + 1)
                nc.gpsimd.tensor_tensor(parts[:, t, low:low + D], work[:, t, :], parts[:, t, low - D:low], ALU.subtract).then_inc(s_parts, 1)

            for i in range(STEPS7):
                low_part(0, i, LOW)
            pool.wait_ge(s_h_table, 16 * STEPS7)
            pool.reg_mov(goal, 1)
            gather(s_staged0, s_gathered0, 0, RAW_GROUPS, h_table, msg0)
            r = is_slow(pool, "pool_slow")
            with pool.If_ne(r, 0):
                gather(s_staged0, s_gathered0, RAW_GROUPS, GROUPS0, h_table, msg0)
            for i in range(STEPS7):
                t = tiles_of_step(i)
                pool.wait_ge(s_h, STEPS7 + i + 1)
                nc.gpsimd.tensor_tensor(xs[:, t, :], xs[:, t, :], h[:, t, :], ALU.add).then_inc(s_residual, 1)
                if i:
                    low_part(1, i - 1, 2 * D)
            low_part(1, STEPS7 - 1, 2 * D)
            for j in range(2):
                pool.wait_ge(s_kv_table[j], 16 * len(range(j, STEPS7, 2)))
            pool.reg_mov(goal, 1)
            gather(s_staged1, s_gathered1, 0, GROUPS1, kv_table, msg)

        @block.scalar
        def _(act):
            copy = nc.scalar.copy

            def square(k, i):
                act.wait_ge(s_centred, k * STEPS7 + i + 1)
                nc.scalar.activation(h[:, tiles_of_step(i), :], work[:, tiles_of_step(i), :], ACT.Square).then_inc(s_squared, 1)

            def deviation(k):
                act.wait_ge(s_var, (k + 1) * STEPS7)
                nc.scalar.activation(stat[:, :], stat2[:, :], ACT.Sqrt, bias=eps_col[:, :], scale=1.0 / D).then_inc(s_sd, 1)

            def transposed_out(k):
                act.wait_ge(s_node_t, k + 1)
                if k >= 2:
                    act.wait_ge(*((s_dense, k - 1) if k < 2 * STEPS7 + 2 else (s_kv_made, k - 2 * STEPS7 - 1)))
                copy(node_t[:, k % 2, :, :], psA[0:D, 0:NT7 * P].rearrange("p (t e) -> p t e", t=NT7)).then_inc(s_node_t_in, 1)

            def mid_part(k, i, mid):
                act.wait_ge(s_rest, k * STEPS7 + i + 1)
                copy(parts[:, tiles_of_step(i), mid:mid + D], work[:, tiles_of_step(i), :]).then_inc(s_mid, 1)

            def stage_cols(b, m, slot):
                copy(cols_stage[:, slot, :, :], cols[:, bass.ds(m * CC, CC), :]).then_inc(b.cols_staged, 1)

            def code_chunk(b, m, slot):
                act.wait_ge(b.cols_staged, m + 1)
                act.wait_ge(b.hot_rows, m + 1)
                act.wait_ge(b.scattered, m + 1)
                for c in range(CC):
                    for part in range(2):
                        last = nc.scalar.mul(code_row[:, slot % 2, c, part, :], hot_row[:, slot % 2, c, :],
                                             cols_stage[:, slot, c, 2 + part:3 + part])
                last.then_inc(b.code_rows, 1)

            def start_codes(b):
                act.wait_ge(b.cols, 1)
                stage_cols(b, 0, 0)
                stage_cols(b, 1, 1)

            def code_steps(b, m, slot):
                code_chunk(b, m, slot)
                copy(cols_stage[:, (slot + 2) % 4, :, :], cols[:, bass.ds(m * CC + 2 * CC, CC), :]).then_inc(b.cols_staged, 1)

            def stage_lists(idx, local, n, u, staged):
                copy(loc_stage[:, u, :], local[:, bass.ds(n * GT, GT)])
                copy(idx_stage[:, u, :], idx[:, bass.ds(n * GT, GT)]).then_inc(staged, 1)

            def restage0(n, u):
                act.wait_ge(s_summed0, n + 1)
                stage_lists(idx0, local0, n + RING, u, s_staged0)

            act.wait_ge(s_const, 1)
            for i in range(STEPS7):
                square(0, i)
            deviation(0)
            for i in range(STEPS7):
                act.wait_ge(s_h, i + 1)
                copy(parts[:, tiles_of_step(i), 0:D], h[:, tiles_of_step(i), :]).then_inc(s_high, 1)
                if i:
                    mid_part(0, i - 1, MID)
            mid_part(0, STEPS7 - 1, MID)
            def stage_first_groups():
                for n in range(RING):
                    stage_lists(idx0, local0, n, n, s_staged0)

            r = is_slow(act, "act_slow")
            act.wait_ge(s_lists0, 1)
            with act.If_eq(r, 0):
                stage_first_groups()
            for i in range(STEPS7):
                transposed_out(i)
            act.wait_ge(s_h_table, 16 * STEPS7)
            with act.If_ne(r, 0):
                start_codes(BK0)
                with act.Fori(0, CHUNKS // 4) as i:
                    for c in range(4):
                        code_steps(BK0, i * 4 + c, c)
                act.wait_ge(BK0.lists, 1)
                stage_first_groups()
            with act.Fori(0, B // RING) as i:
                for u in range(RING):
                    restage0(i * RING + u, u)
            start_codes(BK1)
            code_steps(BK1, 0, 0)
            with act.Fori(B // RING, C // RING) as i:
                for u in range(RING):
                    n = i * RING + u
                    restage0(n, u)
                    code_steps(BK1, n + (1 - B), (u + 1) % 4)
            with act.If_ne(r, 0):
                with act.Fori(C // RING, GROUPS0 // RING) as i:
                    for u in range(RING):
                        restage0(i * RING + u, u)

            for i in range(STEPS7 + 2):
                if i < STEPS7:
                    transposed_out(STEPS7 + i)
                if i >= 2:
                    square(1, i - 2)
            deviation(1)

            transposed_out(2 * STEPS7)
            for i in range(STEPS7):
                if i + 1 < STEPS7:
                    transposed_out(2 * STEPS7 + i + 1)
                act.wait_ge(s_q_made, i + 1)
                for k, (a, b) in enumerate(((0, PER), (PER, NT7))):
                    last = copy(parts[:, i * NT7 + a:i * NT7 + b, 0:D], bank(psB, k)[:, 0:(b - a) * D].rearrange("p (t f) -> p t f", f=D))
                last.then_inc(s_high, 1)
                act.wait_ge(s_kv_made_low, i + 1)
                if i >= 2:
                    act.wait_ge(s_kv_table[i % 2], 16 * (i // 2))
                for k in range(2):
                    last = copy(kv_stage[:, i % 2, 2 * k:2 * k + 2, :], bank(psC, k)[:, 0:4 * D].rearrange("p (t f) -> p t f", f=2 * D))
                last.then_inc(s_kv_low, 1)
                mid_part(1, i, D)

            act.wait_ge(BK1.lists, 1)
            for n in range(RING):
                stage_lists(idx1, local1, n, n, s_staged1)

            def hot_t_out(n, u):
                act.wait_ge(s_hot_t, n + 1)
                wait(act, s_q_edge, n - 1)
                copy(hot_t[:, u % 2, :, :], bank(psA, u % 2).rearrange("p (g e) -> p g e", g=GT)).then_inc(s_hot_t_in, 1)

            def attend_step(n, u):
                act.wait_ge(s_clipped, n + 1)
                wait(act, s_summed1, n - 1)
                nc.scalar.activation(weighted[:, u % 2, :, D:W1],
                                     score[:, u % 2, :].rearrange("p (g h) -> p g h", g=GT), ACT.Exp).then_inc(s_exp, 1)
                hot_t_out(n + 2, u + 2)
                act.wait_ge(s_weighted, n + 1)
                stage_lists(idx1, local1, n + RING, u, s_staged1)

            hot_t_out(0, 0)
            hot_t_out(1, 1)
            rounds(act, GROUPS1, attend_step)

        @block.vector
        def _(dve):
            V = nc.vector
            chain = [0]

            def link(ins, semaphore=s_dve, count=chain):
                count[0] = count[0] + 1
                ins.then_inc(semaphore, 1)
                dve.wait_ge(semaphore, count[0])

            V.memset(raw[:, :, BLK - 1, :], -1).then_inc(s_raw_set, 1)
            V.memset(xs[:, NB - 1, :], 0.0).then_inc(s_x_set, 1)
            V.memset(ones[:, :], 1.0)
            V.memset(ones_h[:, :], 1.0)
            V.memset(zeros_h[:, :], 0.0)
            V.memset(eps_col[:, :], EPS_LN)
            V.memset(parts[:, :, D:MID], 1.0)
            V.memset(parts[:, :, SPLIT - 1:SPLIT], 0.0)
            V.memset(idx1[:, TILES1:], 0)
            V.memset(local1[:, TILES1:], -1.0)
            V.memset(idx0[:, RAWT:], 0)
            V.memset(local0[:, RAWT:], -1.0)
            V.memset(packed1[:, GROUPS1:], 0)
            V.memset(window[:, :, :], 0)
            dve.wait_ge(s_iota, 2)
            V.tensor_copy(iota_part[:, :], iota_part_i[:, :])
            link(V.tensor_copy(iota_f[:, :], iota_i[:, 0:P]))
            V.tensor_copy(iota_b[:, :], iota_i[:, 0:2 * P])
            V.tensor_copy(iota_h[:, :], iota_i[:, :])
            V.tensor_scalar(before[:, :], iota_f[:, :], iota_part[:, :], None, ALU.is_gt)
            V.tensor_scalar(ident[:, :], iota_f[:, :], iota_part[:, :], None, ALU.is_equal).then_inc(s_const, 1)

            over = lambda ap: ap.unsqueeze(2).to_broadcast([P, NT7, D])

            def row_sum(k, i):
                V.tensor_reduce(stat[:, tiles_of_step(i)], xs[:, tiles_of_step(i), :], X, ALU.add).then_inc(s_row_sum, 1)

            def centre(k, i):
                t = tiles_of_step(i)
                dve.wait_ge(s_row_sum, k * STEPS7 + i + 1)
                V.scalar_tensor_tensor(work[:, t, :], over(stat[:, t]), -1.0 / D, xs[:, t, :], ALU.mult, ALU.add).then_inc(s_centred, 1)

            def variance(k, i):
                t = tiles_of_step(i)
                dve.wait_ge(s_squared, k * STEPS7 + i + 1)
                V.tensor_reduce(stat2[:, t], h[:, t, :], X, ALU.add).then_inc(s_var, 1)

            def inverse_deviation(k):
                dve.wait_ge(s_sd, k + 1)
                V.reciprocal(stat2[:, :], stat[:, :]).then_inc(s_rstd, 1)
                dve.wait_ge(s_rstd, k + 1)

            def normalise(i):
                t = tiles_of_step(i)
                V.scalar_tensor_tensor(h[:, t, :], work[:, t, :], 0.0, over(stat2[:, t]), ALU.max, ALU.mult).then_inc(s_h, 1)

            def add_product(k, done):
                i = k % STEPS7
                dve.wait_ge(s_dense, k + 1)
                for j, (a, b) in enumerate(((0, PER), (PER, NT7))):
                    xt = xs[:, i * NT7 + a:i * NT7 + b, :]
                    last = V.tensor_tensor(xt, xt, bank(psC, j)[:, 0:(b - a) * D].rearrange("p (t f) -> p t f", f=D), ALU.add)
                last.then_inc(done, 1)

            dve.wait_ge(s_edges_in, 96)
            V.tensor_copy(raw_f, raw).then_inc(s_raw_f, 1)
            dve.wait_ge(s_raw_f, 1)
            dsts = raw_f[:, 1, :, :]
            tile_ends = base[:, 0:2 * BLK].rearrange("p (k b) -> p k b", k=2)
            filled = scan[:, 0:BLK * P].rearrange("p (b e) -> p b e", b=BLK)
            V.tensor_reduce(tile_ends[:, 0, :], dsts, X, ALU.max)
            link(V.tensor_scalar(filled, dsts, 0.0, float(2 * NPAD), ALU.is_lt, ALU.mult))
            link(V.tensor_tensor(filled, filled, dsts, ALU.add))
            V.tensor_reduce(tile_ends[:, 1, :], filled, X, ALU.min).then_inc(s_tile_ends, 1)
            for k, (e, ps) in enumerate(((edge_src, psB), (edge_dst, psC))):
                dve.wait_ge(s_edge_t, k + 1)
                V.tensor_copy(e[:, :], ps[:, 0:BLK * P]).then_inc(s_edge, 1)
            dve.wait_ge(s_tile_ends_t, 1)
            G = P // GT
            g_max, g_min = position[0:BLK, 0:G], position[0:BLK, G:2 * G]
            gi_max, gi_min = g_window[:, G:2 * G], g_window[:, 0:G]
            V.tensor_reduce(g_max, psD[0:BLK, 0:P].rearrange("p (g t) -> p g t", t=GT), X, ALU.max)
            link(V.tensor_reduce(g_min, psD[0:BLK, P:2 * P].rearrange("p (g t) -> p g t", t=GT), X, ALU.min))
            V.tensor_copy(gi_max, g_max)
            link(V.tensor_copy(gi_min, g_min))
            V.tensor_scalar(gi_max, gi_max, 7, None, ALU.arith_shift_right)
            link(V.tensor_scalar(gi_min, gi_min, 7, None, ALU.arith_shift_right))
            link(V.tensor_scalar(gi_min, gi_min, NB - 1.0, None, ALU.min))
            link(V.tensor_tensor(g_max, gi_max, gi_min, ALU.subtract))
            V.tensor_scalar(gi_max, g_max, 0.0, None, ALU.is_gt).then_inc(s_windows, 1)
            link(V.tensor_reduce(g_min[:, 0:1], g_max, X, ALU.max))
            V.tensor_scalar(g_span, g_min[:, 0:1], 1.0, None, ALU.is_gt).then_inc(s_windows, 1)
            dve.wait_ge(s_window_all, 1)
            V.tensor_scalar(slow[:, :], psD[0:1, HALF:HALF + 1], 1.0, None, ALU.mult).then_inc(s_wide, 1)
            for i in range(STEPS7 + 3):
                for c, (a, b) in enumerate(LOADS):
                    if i == a:
                        dve.wait_ge(s_x_in[c], 32 if b == STEPS7 else 16)
                if i < STEPS7:
                    row_sum(0, i)
                if 1 <= i <= STEPS7:
                    centre(0, i - 1)
                if i >= 3:
                    variance(0, i - 3)
            dve.wait_ge(s_w_t, 1)
            V.tensor_copy(w_in[:, :, :], psA[0:D, 0:2 * D].rearrange("p (w f) -> p w f", w=2)).then_inc(s_w_ready, 1)
            inverse_deviation(0)
            normalise(0)
            for i in range(STEPS7):
                if i + 1 < STEPS7:
                    normalise(i + 1)
                t = tiles_of_step(i)
                dve.wait_ge(s_high, i + 1)
                V.tensor_tensor(work[:, t, :], h[:, t, :], parts[:, t, 0:D], ALU.subtract).then_inc(s_rest, 1)

            dve.wait_ge(s_window_row, 32)
            V.tensor_copy(scan[0:1, 0:BLK * G], window[0:1, 0, 0:BLK * G]).then_inc(s_window_f, 1)
            V.scalar_tensor_tensor(window[0:1, 0, 0:BLK * G], window[0:1, 1, 0:BLK * G], float(NEXT), window[0:1, 0, 0:BLK * G], ALU.mult, ALU.add)
            V.tensor_scalar(idx0[:, 0:RAWT], edge_src[:, 0:RAWT], 0.0, None, ALU.max)
            dve.wait_ge(s_window_all, 2)
            V.scalar_tensor_tensor(
                local0[:, 0:RAWT].rearrange("p (g t) -> p g t", t=GT),
                psD[:, 0:RAW_GROUPS].unsqueeze(2).to_broadcast([P, RAW_GROUPS, GT]), -float(P),
                edge_dst[:, 0:RAWT].rearrange("p (g t) -> p g t", t=GT), ALU.mult, ALU.add).then_inc(s_lists0, 1)

            half = NB // 2
            V.memset(acc[:, 0:half, :], 0.0).then_inc(s_added0, 1)
            V.memset(acc[:, half:, :], 0.0).then_inc(s_added0, 1)

            def count_bucket(b, k, to):
                return V.tensor_scalar(to, bucket[:, :], iota_f[:, bass.ds(k, 1)], None, ALU.is_equal, ALU.add,
                                       accum_out=counts[:, bass.ds(k, 1)])

            def bucket_starts(b, do):
                V.tensor_copy(units_f[:, :], counts[:, :]).then_inc(b.counts, 1)
                dve.wait_ge(b.totals, 1)
                do(V.tensor_scalar(units_i[:, :], psD[:, NB:2 * NB], float((1 << b.unit_shift) - 1), None, ALU.add))
                do(V.tensor_scalar(units_i[:, :], units_i[:, :], b.unit_shift, None, ALU.arith_shift_right))
                do(V.tensor_copy(units_f[:, :], units_i[:, :]))
                V.tensor_tensor_scan(units_end[:, :], ones[:, 0:NB], units_f[:, :], 0.0, ALU.mult, ALU.add).then_inc(b.units_end, 1)
                dve.wait_ge(b.units_end, 1)
                do(V.tensor_tensor(base[:, :], units_end[:, :], units_f[:, :], ALU.subtract))
                do(V.scalar_tensor_tensor(base[:, :], base[:, :], float(1 << b.unit_shift), psD[:, 0:NB], ALU.mult, ALU.add))
                dve.wait_ge(b.end_t, 1)
                do(V.tensor_copy(end_col[0:NB, :], psD[0:NB, HALF:HALF + 1]))
                V.tensor_scalar(past_end[0:NB, 0:b.units], iota_h[0:NB, 0:b.units], end_col[0:NB, :], None, ALU.is_ge).then_inc(b.past_end, 1)

            def unit_buckets(b, do):
                dve.wait_ge(b.unit_bucket_sum, 1)
                do(V.tensor_scalar(b.unit_bucket[:, 0:b.units], psC[0:1, 0:b.units], NB - 1.0, None, ALU.min))

            places = lambda k: (psA, psC)[k % 2][:, 0:COLS]

            def mask_bucket(b, k, slot):
                V.tensor_scalar(mask[:, slot % 4, :], bucket[:, :], iota_f[:, bass.ds(k, 1)], None, ALU.is_equal).then_inc(b.place, 1)

            def scan_bucket(b, k, slot):
                dve.wait_ge(b.place, k + 1)
                V.tensor_tensor_scan(places(slot), ones[:, 0:1].to_broadcast([P, COLS]), mask[:, slot % 4, :],
                                     base[:, bass.ds(k, 1)], ALU.mult, ALU.add)

            def copy_places(slot):
                return V.copy_predicated(position[:, :], mask[:, slot % 4, :].bitcast(u16), places(slot))

            def place_first(b):
                mask_bucket(b, 0, 0)
                scan_bucket(b, 0, 0)
                mask_bucket(b, 1, 1)

            def place_bucket(b, k, slot):
                scan_bucket(b, k, slot)
                copy_places(slot - 1)
                mask_bucket(b, k + 1, slot + 1)

            def place_last(b, do):
                dve.wait_ge(b.place, NB + 1)
                do(copy_places(NB - 1))

            def rows_and_tiles(b, do):
                wi = ints[:, 0:COLS]
                do(V.tensor_scalar(position[:, :], position[:, :], -1.0, None, ALU.add))
                do(V.tensor_copy(wi, position[:, :]))
                do(V.tensor_scalar(wi, wi, 7, None, ALU.arith_shift_right))
                do(V.tensor_copy(cols[:, 0:COLS, 1], wi))
                V.scalar_tensor_tensor(cols[:, 0:COLS, 0], cols[:, 0:COLS, 1], -float(P), position[:, :], ALU.mult, ALU.add).then_inc(b.code_rows, 2)
                V.memset(cols[:, COLS:, :], 0.0).then_inc(b.cols, 1)

            def hot_rows(b, m, slot):
                dve.wait_ge(b.cols_staged, m + 1)
                dve.wait_ge(b.code_rows, m + 1)
                for c in range(CC):
                    last = V.tensor_scalar(hot_row[:, slot % 2, c, :], iota_h[:, 0:P], cols_stage[:, slot, c, 0:1], None, ALU.is_equal)
                last.then_inc(b.hot_rows, 1)

            def hot_tiles(b, m, slot):
                dve.wait_ge(b.scattered, m + 1)
                for c in range(CC):
                    last = V.tensor_scalar(hot_tile[:, slot % 2, c, 0:b.tiles], iota_h[:, 0:b.tiles], cols_stage[:, slot, c, 1:2], None, ALU.is_equal)
                last.then_inc(b.hot_tiles, 1)

            def decode(b, staged, do):
                code = scan[:, 0:b.tiles].bitcast(i32)
                wi = ints[:, 0:b.tiles]
                dve.wait_ge(b.code, 1)
                dve.wait_ge(b.cols_staged, staged)
                do(V.tensor_scalar(code, psA[:, 0:b.tiles], 1024.0, None, ALU.mult))
                do(V.tensor_scalar(wi, code, 13, None, ALU.arith_shift_right))
                V.tensor_scalar(b.other_idx[:, 0:b.tiles], code, 8191, None, ALU.bitwise_and)
                V.tensor_scalar(b.local[:, 0:b.tiles], wi, -1.0, None, ALU.add).then_inc(b.lists, 1)

            def codes(b, do):
                keys, others = b.key[:, 0:COLS], b.other[:, 0:COLS]
                w, wi = scan[:, 0:COLS], ints[:, 0:COLS]
                do(V.tensor_copy(wi, keys))
                do(V.tensor_scalar(wi, wi, 7, None, ALU.arith_shift_right))
                do(V.tensor_copy(bucket[:, :], wi))
                do(V.tensor_copy(wi, others))
                do(V.tensor_scalar(wi, wi, 10, None, ALU.arith_shift_right))
                do(V.tensor_copy(position[:, :], wi))
                do(V.scalar_tensor_tensor(w, position[:, :], -1024.0, others, ALU.mult, ALU.add))
                do(V.tensor_scalar(cols[:, 0:COLS, 3], w, 1.0 / 1024.0, None, ALU.mult))
                do(V.scalar_tensor_tensor(w, bucket[:, :], -float(P), keys, ALU.mult, ALU.add))
                do(V.tensor_scalar(w, w, 1.0, 8.0, ALU.add, ALU.mult))
                do(V.tensor_tensor(cols[:, 0:COLS, 2], w, position[:, :], ALU.add))
                do(V.memset(position[:, :], 0.0))

            def make_hot0(n, u):
                dve.wait_ge(s_staged0, n + 1)
                for g in range(GT):
                    ins = V.tensor_scalar(hot0[:, u % RING, g, :], iota_b[:, :], loc_stage[:, u % RING, g:g + 1], None, ALU.is_equal)
                    if g == 0:
                        ins.then_inc(s_added0, 1)
                ins.then_inc(s_hot0, 1)

            r = is_slow(dve, "dve_slow")
            dve.wait_ge(s_lists0, 1)
            with dve.If_eq(r, 0):
                make_hot0(0, 0)
            dve.wait_ge(s_h_table, 16 * STEPS7)
            steps = iter(range(STEPS7))

            def link_beside_product(ins):
                link(ins)
                i = next(steps, None)
                if i is not None:
                    add_product(i, s_x_self)
            codes(BK1, link_beside_product)
            with dve.If_ne(r, 0):
                chain0 = [0]
                do = lambda ins: link(ins, BK0.step, chain0)
                codes(BK0, do)
                start = chain0[0]
                with dve.Fori(0, NB) as k:
                    chain0[0] = k * 1 + start
                    do(count_bucket(BK0, k, hot_tile[:, 0, 0, 0:COLS]))
                chain0[0] = start + NB
                bucket_starts(BK0, do)
                unit_buckets(BK0, do)
                do(V.memset(window[:, 1, :], 0))
                place_first(BK0)
                with dve.Fori(0, NB // 4) as i:
                    for c in range(4):
                        place_bucket(BK0, i * 4 + (1 + c), 1 + c)
                place_last(BK0, do)
                rows_and_tiles(BK0, do)
                with dve.Fori(0, CHUNKS // 4) as i:
                    for c in range(4):
                        hot_rows(BK0, i * 4 + c, c)
                        hot_tiles(BK0, i * 4 + c, c)
                decode(BK0, CHUNKS + 2, do)
                dve.wait_ge(BK0.lists, 1)
                codes(BK1, do)
                make_hot0(0, 0)

            window_reg = dve.alloc_register("window")
            first_bucket = dve.alloc_register("first_bucket")
            two_buckets = dve.alloc_register("two_buckets")

            def load_window(n):
                dve.reg_load(window_reg, window[0:1, 0, bass.ds(n, 1)])

            def add0(n, u):
                dve.reg_alu(first_bucket, window_reg, NEXT - 1, ALU.bitwise_and)
                dve.reg_alu(two_buckets, window_reg, NEXT, ALU.bitwise_and)
                w = dve.snap(first_bucket, min_val=0, max_val=NB - 1)
                dve.wait_ge(s_summed0, n + 1)
                dve.wait_ge(s_added0, n + 3)
                sums = flat(acc[:, bass.ds(w, 1), 0:W0])
                V.tensor_tensor(sums, sums, bank(psB, u % 2)[:, 0:W0], ALU.add)
                with dve.If_ne(two_buckets, 0):
                    sums = flat(acc[:, bass.ds(w + 1, 1), 0:W0])
                    V.tensor_tensor(sums, sums, bank(psB, u % 2)[:, P:P + W0], ALU.add)

            def group_steps(lo, hi, beside, before=lambda n, u: None):
                with dve.Fori(lo // RING, hi // RING) as i:
                    for u in range(RING):
                        n = i * RING + u
                        before(n, u)
                        add0(n, u)
                        make_hot0(n + 1, u + 1)
                        load_window(n + 1)
                        beside(n, u)

            load_window(0)

            def counts_beside(n, u):
                for c in range(A_COUNTS):
                    count_bucket(BK1, n * A_COUNTS + (1 + c), hot_tile[:, u % 2, c, 0:COLS])
            group_steps(0, A, counts_beside)
            link(count_bucket(BK1, 0, hot_tile[:, 0, A_COUNTS, 0:COLS]))
            bucket_starts(BK1, link)
            unit_buckets(BK1, link)
            tiles_of = bucket1[:, :].rearrange("o (g t) -> o g t", t=GT)
            packed = packed1[:, 0:GROUPS1]
            link(V.scalar_tensor_tensor(packed, tiles_of[:, :, 3], float(NEXT), tiles_of[:, :, 2], ALU.mult, ALU.add))
            link(V.scalar_tensor_tensor(packed, packed, float(NEXT), tiles_of[:, :, 1], ALU.mult, ALU.add))
            link(V.scalar_tensor_tensor(packed, packed, float(NEXT), tiles_of[:, :, 0], ALU.mult, ALU.add))
            place_first(BK1)
            with dve.Fori(A // RING, B // RING) as i:
                for u in range(RING):
                    n = i * RING + u
                    add0(n, u)
                    make_hot0(n + 1, u + 1)
                    load_window(n + 1)
                    for c in range(B_PLACED):
                        place_bucket(BK1, n * B_PLACED + (1 + c - B_PLACED * A), u * B_PLACED + 1 + c)
            place_last(BK1, link)
            rows_and_tiles(BK1, link)

            hot_rows(BK1, 0, 0)
            hot_tiles(BK1, 0, 0)
            group_steps(B, C, lambda n, u: hot_tiles(BK1, n + (1 - B), (u + 1) % 4),
                        before=lambda n, u: hot_rows(BK1, n + (1 - B), (u + 1) % 4))
            with dve.If_ne(r, 0):
                group_steps(C, GROUPS0, lambda n, u: None)
            deg = acc[:, 0:NB, D:W0].rearrange("p t o -> p (t o)")
            link(V.memset(stat[:, :], 0.0))
            link(V.tensor_scalar(stat[:, :], deg, EPS, None, ALU.add))
            link(V.reciprocal(stat2[:, :], stat[:, :]))
            decode(BK1, CHUNKS + 3, link)
            dve.wait_ge(BK1.lists, 1)


            def mean(i):
                t = tiles_of_step(i)
                V.scalar_tensor_tensor(work[:, t, :], acc[:, t, 0:D], EPS, over(stat2[:, t]), ALU.add, ALU.mult).then_inc(s_mean, 1)

            mean(0)
            mean(1)
            for i in range(STEPS7 + 3):
                if i + 2 < STEPS7:
                    mean(i + 2)
                if i < STEPS7:
                    add_product(STEPS7 + i, s_x1)
                if 1 <= i <= STEPS7:
                    centre(1, i - 1)
                if i < STEPS7:
                    dve.wait_ge(s_x1, i + 1)
                    row_sum(1, i)
                if i >= 3:
                    variance(1, i - 3)
            inverse_deviation(1)
            normalise(0)
            normalise(1)
            for i in range(STEPS7):
                if i + 2 < STEPS7:
                    normalise(i + 2)
                dve.wait_ge(s_high, STEPS7 + i + 1)
                for k, (a, b) in enumerate(((0, PER), (PER, NT7))):
                    t = slice(i * NT7 + a, i * NT7 + b)
                    last = V.tensor_tensor(work[:, t, :], bank(psB, k)[:, 0:(b - a) * D].rearrange("p (t f) -> p t f", f=D), parts[:, t, 0:D], ALU.subtract)
                last.then_inc(s_rest, 1)
                dve.wait_ge(s_kv_made, i + 1)
                if i >= 2:
                    dve.wait_ge(s_kv_table[i % 2], 16 * (i // 2))
                for k in range(2):
                    a, b = 2 * k + 4, min(2 * k + 6, NT7)
                    last = V.tensor_copy(kv_stage[:, i % 2, a:b, :], bank(psD, k)[:, 0:(b - a) * 2 * D].rearrange("p (t f) -> p t f", f=2 * D))
                last.then_inc(s_kv_high, 1)

            link(V.memset(acc[:, :, :], 0.0))
            tile_regs = [dve.alloc_register(f"tile_bucket{g}") for g in range(GT)]

            def hot1_tile(n, u, g):
                if g == 0:
                    dve.wait_ge(s_staged1, n + 1)
                ins = V.tensor_scalar(hot[:, u % RING, g, :], iota_f[:, :], loc_stage[:, u % RING, g:g + 1], None, ALU.is_equal)
                if g == GT - 1:
                    ins.then_inc(s_hot1, 1)

            def add1_tile(n, u, g):
                b = dve.snap(tile_regs[g], min_val=0, max_val=NB - 1)
                sums = flat(acc[:, bass.ds(b, 1), :])
                if g == 0:
                    dve.wait_ge(s_summed1, n + 1)
                wait(dve, s_added1, n * GT + g)
                V.tensor_tensor(sums, sums, bank(psC, u % 2)[:, g * W1:(g + 1) * W1], ALU.add).then_inc(s_added1, 1)

            packed_reg = dve.alloc_register("packed")

            def load_buckets(n):
                dve.reg_load(packed_reg, packed1[0:1, bass.ds(n, 1)])

            LINKS1 = 2

            def attend_step(n, u):
                first = isinstance(n, int) and n < 2
                dve.wait_ge(s_q_edge, n + 1)
                dve.wait_ge(s_gathered1[u], arrived(n, u))
                ins = V.tensor_tensor(prod[:, :, :], bank(psB, u % 2)[:, 0:GT * D].rearrange("p (g f) -> p g f", g=GT),
                                      msg[:, u, :, 0:D], ALU.mult)
                if not first:
                    load_buckets(n - 2)
                link(ins)
                ins = V.tensor_reduce(score[:, u % 2, :], prod[:, :, :].rearrange("p g (h d) -> p (g h) d", d=DH), X, ALU.add)
                if not first:
                    unpack(dve, tile_regs, packed_reg)
                link(ins)
                V.tensor_scalar(score[:, u % 2, :], score[:, u % 2, :], -10.0, 10.0, ALU.max, ALU.min).then_inc(s_clipped, 1)
                wait(dve, s_summed1, n)
                for g in range(GT):
                    hot1_tile(n + 3, u + 3, g)
                    if not first:
                        add1_tile(n - 2, u - 2, g)
                dve.wait_ge(s_exp, n + 1)
                wait(dve, s_summed1, n - 1)
                V.tensor_tensor(weighted[:, u % 2, :, 0:D].rearrange("p g (h d) -> p g h d", h=HEADS),
                                msg[:, u, :, D:2 * D].rearrange("p g (h d) -> p g h d", h=HEADS),
                                weighted[:, u % 2, :, D:W1].unsqueeze(3).to_broadcast([P, GT, HEADS, DH]),
                                ALU.mult).then_inc(s_weighted, 1)

            def arrived(n, u):
                return (n - u) * (16 * GT // RING) + 16 * GT

            dve.wait_ge(s_kv_high, STEPS7)
            dve.wait_ge(s_kv_low, STEPS7)
            for g in range(GT):
                hot1_tile(0, 0, g)
            for g in range(GT):
                hot1_tile(1, 1, g)
            for g in range(GT):
                hot1_tile(2, 2, g)
            start = chain[0]
            for n in range(RING):
                attend_step(n, n)
            with dve.Fori(1, GROUPS1 // RING) as i:
                chain[0] = i * (LINKS1 * RING) + start
                for u in range(RING):
                    attend_step(i * RING + u, u)
            chain[0] = start + LINKS1 * GROUPS1
            for n in (GROUPS1 - 2, GROUPS1 - 1):
                load_buckets(n)
                unpack(dve, tile_regs, packed_reg)
                for g in range(GT):
                    add1_tile(n, n % RING, g)
            dve.wait_ge(s_added1, TILES1)
            link(V.tensor_scalar(rec[:, :, :], acc[:, 0:NB, D:W1], EPS, None, ALU.add))
            link(V.reciprocal(rec[:, :, :], rec[:, :, :]))
            dve.wait_ge(s_residual, STEPS7)
            by_head = lambda t: t.rearrange("p t (h d) -> p t h d", h=HEADS)

            def scale_sums(i):
                t = tiles_of_step(i)
                link(V.tensor_tensor(by_head(work[:, t, :]), by_head(acc[:, t, 0:D]),
                                     rec[:, t, :].unsqueeze(3).to_broadcast([P, NT7, HEADS, DH]), ALU.mult))

            for i in range(STEPS7):
                scale_sums(i)
                t = tiles_of_step(i)
                V.tensor_tensor(work[:, t, :], work[:, t, :], xs[:, t, :], ALU.add).then_inc(s_out_ready, 1)

        @block.tensor
        def _(pe):
            mm = nc.tensor.matmul
            T = nc.tensor.transpose
            pe.wait_ge(s_const, 1)
            pe.wait_ge(s_raw_f, 1)
            for k, ps in ((0, psB), (1, psC)):
                for b in range(BLK):
                    last = T(ps[:, b * P:(b + 1) * P], raw_f[:, k, b, :], ident[:, :])
                last.then_inc(s_edge_t, 1)
            pe.wait_ge(s_tile_ends, 1)
            for k in range(2):
                last = T(psD[0:BLK, k * P:(k + 1) * P], base[:, k * BLK:(k + 1) * BLK], ident[:, :])
            last.then_inc(s_tile_ends_t, 1)
            pe.wait_ge(s_windows, 2)
            mm(psD[0:1, HALF:HALF + 1], ones[0:BLK, 0:1], g_span, start=True, stop=True).then_inc(s_window_all, 1)
            pe.wait_ge(s_w_in, 80)
            for k in range(2):
                last = T(psA[0:D, k * D:(k + 1) * D], w_rows[:, k, :], ident[0:D, 0:D])
            last.then_inc(s_w_t, 1)
            pe.wait_ge(s_window_f, 1)
            mm(psD[:, 0:BLK * P // GT], ones[0:1, :], scan[0:1, 0:BLK * P // GT], start=True, stop=True).then_inc(s_window_all, 1)

            def transpose_step(k, made, i, source):
                pe.wait_ge(made, i + 1)
                wait(pe, s_node_t_in, k)
                for t in range(NT7):
                    last = T(psA[0:D, t * P:(t + 1) * P], source[:, k % STEPS7 * NT7 + t, :], ident[:, :])
                last.then_inc(s_node_t, 1)

            def product_of_steps(k, made, source, weights, added):
                transpose_step(k, made, 0, source)
                for i in range(STEPS7):
                    if i + 1 < STEPS7:
                        transpose_step(k + i + 1, made, i + 1, source)
                    pe.wait_ge(s_node_t_in, k + i + 1)
                    wait(pe, added, i)
                    for t in range(NT7):
                        last = mm(bank(psC, t // PER)[:, (t % PER) * D:(t % PER + 1) * D], node_t[:, (k + i) % 2, t, :], weights,
                                  start=True, stop=True)
                    last.then_inc(s_dense, 1)

            pe.wait_ge(s_w_ready, 1)
            product_of_steps(0, s_h, h, w_in[:, 0, :], s_x_self)

            def bucket_totals(b):
                pe.wait_ge(b.counts, 1)
                mm(psD[:, 0:NB], before[:, :], counts[:, :], start=True, stop=True)
                mm(psD[:, NB:2 * NB], ones[:, :], counts[:, :], start=True, stop=True).then_inc(b.totals, 1)
                pe.wait_ge(b.units_end, 1)
                mm(psD[0:NB, HALF:HALF + 1], units_end[0:1, :], ones[0:1, 0:1], start=True, stop=True).then_inc(b.end_t, 1)
                pe.wait_ge(b.past_end, 1)
                for lo, hi in halves(b.units):
                    last = mm(psC[0:1, lo:hi], ones_h[0:NB, :], past_end[0:NB, lo:hi], start=True, stop=True)
                last.then_inc(b.unit_bucket_sum, 1)

            def start_scatter(b):
                pe.wait_ge(b.cols, 1)
                for lo, hi in halves(b.tiles):
                    mm(psA[:, lo:hi], zeros_h[:, :], iota_h[:, lo:hi], start=True, stop=False).then_inc(b.scattered, 1)

            def scatter_chunk(b, m, slot):
                pe.wait_ge(b.hot_tiles, m + 1)
                pe.wait_ge(b.code_rows, m + 3)
                for c in range(CC):
                    for part in range(2):
                        for lo, hi in halves(b.tiles):
                            last = mm(psA[:, lo:hi], code_row[:, slot % 2, c, part, :], hot_tile[:, slot % 2, c, lo:hi],
                                      start=False, stop=False)
                last.then_inc(b.scattered, 1)

            def end_scatter(b):
                for lo, hi in halves(b.tiles):
                    last = mm(psA[:, lo:hi], zeros_h[:, :], iota_h[:, lo:hi], start=False, stop=True)
                last.then_inc(b.code, 1)

            r = is_slow(pe, "pe_slow")
            with pe.If_ne(r, 0):
                bucket_totals(BK0)
                start_scatter(BK0)
                with pe.Fori(0, CHUNKS // 4) as i:
                    for c in range(4):
                        scatter_chunk(BK0, i * 4 + c, c)
                end_scatter(BK0)
                pe.wait_ge(BK0.lists, 1)
            pe.wait_ge(s_lists0, 1)

            two_buckets = pe.alloc_register("pe_two_buckets")

            def sum0_half(n, u, half):
                o = bank(psB, u % 2)[:, half * P:half * P + W0]
                for g in range(GT):
                    for k, (lo, hi) in enumerate(((0, W0), (MID, MID + D), (LOW, LOW + D))):
                        last = mm(o[:, 0:hi - lo], hot0[:, u, g, half * P:(half + 1) * P], msg0[:, u, g, lo:hi],
                                  start=(g == 0 and k == 0), stop=(g == GT - 1 and k == 2))
                return last

            def sum_group0(n, u):
                pe.reg_load(two_buckets, window[0:1, 1, bass.ds(n, 1)])
                pe.wait_ge(s_hot0, n + 1)
                pe.wait_ge(s_gathered0[u], (n - u) * (16 * GT // RING) + 16 * GT)
                pe.wait_ge(s_added0, n + 2)
                with pe.If_ne(two_buckets, 0):
                    sum0_half(n, u, 1)
                sum0_half(n, u, 0).then_inc(s_summed0, 1)

            with pe.Fori(0, A // RING) as i:
                for u in range(RING):
                    sum_group0(i * RING + u, u)
            bucket_totals(BK1)
            with pe.Fori(A // RING, B // RING) as i:
                for u in range(RING):
                    sum_group0(i * RING + u, u)
            start_scatter(BK1)
            with pe.Fori(B // RING, C // RING) as i:
                for u in range(RING):
                    n = i * RING + u
                    sum_group0(n, u)
                    scatter_chunk(BK1, n - B, u)
            end_scatter(BK1)
            with pe.If_ne(r, 0):
                with pe.Fori(C // RING, GROUPS0 // RING) as i:
                    for u in range(RING):
                        sum_group0(i * RING + u, u)

            pe.wait_ge(BK1.lists, 1)

            product_of_steps(STEPS7, s_mean, work, w_in[:, 1, :], s_x1)

            transpose_step(2 * STEPS7, s_h, STEPS7, h)
            for i in range(STEPS7):
                if i + 1 < STEPS7:
                    transpose_step(2 * STEPS7 + i + 1, s_h, STEPS7 + i + 1, h)
                pe.wait_ge(s_node_t_in, 2 * STEPS7 + i + 1)
                pe.wait_ge(s_rest, STEPS7 + i)
                for t in range(NT7):
                    last = mm(bank(psB, t // PER)[:, (t % PER) * D:(t % PER + 1) * D], node_t[:, (2 * STEPS7 + i) % 2, t, :], w_qkv[:, 0:D], start=True, stop=True)
                last.then_inc(s_q_made, 1)
                wait(pe, s_kv_low, i)
                for t in range(NT7):
                    if t == 4:
                        last.then_inc(s_kv_made_low, 1)
                        wait(pe, s_kv_high, i)
                    last = mm(bank(psC if t < 4 else psD, t // 2 % 2)[:, (t % 2) * 2 * D:(t % 2 + 1) * 2 * D], node_t[:, (2 * STEPS7 + i) % 2, t, :],
                              w_qkv[:, D:3 * D], start=True, stop=True)
                last.then_inc(s_kv_made, 1)

            q_packed = pe.alloc_register("q_packed")
            q_regs = [pe.alloc_register(f"q_bucket{g}") for g in range(GT)]

            def load_q_buckets(n):
                pe.reg_load(q_packed, packed1[0:1, bass.ds(n, 1)])
                unpack(pe, q_regs, q_packed)

            def transpose_hot(n, u):
                pe.wait_ge(s_hot1, n + 1)
                wait(pe, s_hot_t_in, n - 1)
                for g in range(GT):
                    last = T(bank(psA, u % 2)[:, g * P:(g + 1) * P], hot[:, u % RING, g, :], ident[:, :])
                last.then_inc(s_hot_t, 1)

            def q_of_edges(n, u):
                pe.wait_ge(s_hot_t_in, n + 1)
                wait(pe, s_clipped, n - 1)
                for g in range(GT):
                    b = pe.snap(q_regs[g], min_val=0, max_val=NB - 1)
                    for k in range(3):
                        last = mm(bank(psB, u % 2)[:, g * D:(g + 1) * D], hot_t[:, u % 2, g, :],
                                  flat(parts[:, bass.ds(b, 1), k * D:(k + 1) * D]), start=(k == 0), stop=(k == 2))
                last.then_inc(s_q_edge, 1)

            def sum_weighted(n, u):
                pe.wait_ge(s_weighted, n + 1)
                wait(pe, s_added1, (n - 1) * GT)
                for g in range(GT):
                    last = mm(bank(psC, u % 2)[:, g * W1:(g + 1) * W1], hot[:, u, g, :], weighted[:, u % 2, g, :], start=True, stop=True)
                last.then_inc(s_summed1, 1)

            transpose_hot(0, 0)
            transpose_hot(1, 1)
            pe.wait_ge(s_parts, 2 * STEPS7)
            load_q_buckets(0)
            q_of_edges(0, 0)
            transpose_hot(2, 2)
            load_q_buckets(1)
            q_of_edges(1, 1)
            load_q_buckets(2)

            def attend_step(n, u):
                sum_weighted(n, u)
                q_of_edges(n + 2, u + 2)
                transpose_hot(n + 3, u + 3)
                load_q_buckets(n + 3)
            rounds(pe, GROUPS1, attend_step)


def kernel(x, src, dst, L0_gnn_W_self, L0_gnn_W_neigh, L1_gnn_qW, L1_gnn_kW, L1_gnn_vW):
    import numpy as np
    import concourse.bacc as bacc
    from concourse.bass_utils import run_bass_kernel_spmd

    nc = bacc.Bacc("TRN2", target_bir_lowering=False, num_devices=1)
    given = dict(x=x, src=src, dst=dst, w_self=L0_gnn_W_self, w_neigh=L0_gnn_W_neigh, qw=L1_gnn_qW, kw=L1_gnn_kW, vw=L1_gnn_vW)
    arrays, args = {}, []
    for name, a in given.items():
        a = np.ascontiguousarray(a)
        arrays["in_" + name] = a
        args.append(nc.dram_tensor("in_" + name, a.shape, mybir.dt.from_np(a.dtype), kind="ExternalInput").ap())
    h_table = nc.dram_tensor("h_table", (NPAD, SPLIT), mybir.dt.bfloat16, kind="Internal").ap()
    kv_table = nc.dram_tensor("kv_table", (NPAD, 2 * D), mybir.dt.float32, kind="Internal").ap()
    out = nc.dram_tensor("out", (N_NODES, D), mybir.dt.float32, kind="ExternalOutput").ap()
    gnn_program(nc, *args, h_table, kv_table, out)
    r = run_bass_kernel_spmd(nc, [arrays], core_ids=[0])
    return r.results[0]["out"]
```
